# Optimizing a Trainium2 kernel written in Bass

```python
import numpy as np
import jax
import jax.numpy as jnp

def _softmax(x, axis=-1):
    return jax.nn.softmax(x, axis=axis)

def _gelu(x):
    return jax.nn.gelu(x, approximate=True)

def _silu(x):
    return jax.nn.silu(x)

def _sigmoid(x):
    return jax.nn.sigmoid(x)

def _layernorm(x, axis=-1, eps=1e-05):
    m = jnp.mean(x, axis=axis, keepdims=True)
    v = jnp.var(x, axis=axis, keepdims=True)
    return (x - m) / jnp.sqrt(v + eps)

def _scatter_add(tgt, idx, src, axis=0):
    return tgt.at[idx].add(src)

def _segment_sum(src, seg, n):
    return jax.ops.segment_sum(src, seg, n)
kernel_name = 'mk_metaformer_d1_conv_nchw256_r2_3c3033'

def setup_inputs(seed: int=0):
    np.random.seed(seed)
    _w = jnp.asarray

    def _rec_inputs():
        import jax
        import jax.numpy as jnp
        _gk = jax.random.key(seed)
        x = 1.167e-05 + 1 * jax.random.normal(jax.random.fold_in(_gk, 1), (1, 128, 40, 40), jnp.float32)
        return x
    x = _rec_inputs()

    def _L0_conv_setup():
        import jax, jax.numpy as jnp
        import numpy as np
        DIM = 128
        HEADS = 8
        SIZE = 40
        K = 17
        PAD = K // 2
        K2 = K * K

        def _unfold(img, k):
            B, C = (img.shape[0], img.shape[1])
            p = jax.lax.conv_general_dilated_patches(img, (k, k), (1, 1), 'VALID')
            return p.reshape(B, C * k * k, -1)
        key = jax.random.key(seed)
        ks = jax.random.split(key, 4)
        x = jax.random.normal(ks[0], (1, DIM, SIZE, SIZE), dtype=jnp.float32)
        w_qkv = jax.random.normal(ks[1], (3 * DIM, DIM), dtype=jnp.float32) * 0.05
        b_qkv = jnp.zeros((3 * DIM,), dtype=jnp.float32)
        w_proj = jax.random.normal(ks[2], (DIM, DIM), dtype=jnp.float32) * 0.05
        b_proj = jnp.zeros((DIM,), dtype=jnp.float32)
        return {'x': x, 'w_qkv': w_qkv, 'b_qkv': b_qkv, 'w_proj': w_proj, 'b_proj': b_proj}
    _L0_conv_all = _L0_conv_setup()
    _L0_conv_in = {k: v for k, v in _L0_conv_all.items() if k in ('w_qkv', 'b_qkv', 'w_proj', 'b_proj')}
    del _L0_conv_all

    def _L0_ffn_setup():
        import jax, jax.numpy as jnp
        import numpy as np
        NUM_EXPERTS = 8
        TOP_K = 2
        B, S, D = (8, 4096, 128)

        def _moe(tokens, router_w, w1, b1, w2, b2):
            N = tokens.shape[0]
            E = router_w.shape[0]
            logits = tokens.astype(jnp.float32) @ router_w.astype(jnp.float32).T
            probs = jax.nn.softmax(logits, axis=-1)
            rw, re = jax.lax.top_k(probs, TOP_K)
            if TOP_K > 1:
                rw = rw / jnp.maximum(rw.sum(-1, keepdims=True), 1e-12)
            rw = rw.astype(tokens.dtype)
            combine = jnp.zeros((N, E), tokens.dtype).at[jnp.arange(N)[:, None], re].set(rw)
            out = tokens
            for e in range(E):
                h = jax.nn.gelu(tokens @ w1[e] + b1[e], approximate=False)
                y = h @ w2[e] + b2[e]
                out = out + combine[:, e:e + 1] * y
            return out
        key = jax.random.key(seed)
        ks = jax.random.split(key, 4)
        scale = 1.0 / np.sqrt(D).astype(np.float32)
        return {'input_embeddings': jax.random.normal(ks[0], (B, S, D), jnp.float32), 'router_w': jax.random.normal(ks[1], (NUM_EXPERTS, D), jnp.float32) * scale, 'w1': jax.random.normal(ks[2], (NUM_EXPERTS, D, D), jnp.float32) * scale, 'b1': jnp.zeros((NUM_EXPERTS, D), jnp.float32), 'w2': jax.random.normal(ks[3], (NUM_EXPERTS, D, D), jnp.float32) * scale, 'b2': jnp.zeros((NUM_EXPERTS, D), jnp.float32)}
    _L0_ffn_all = _L0_ffn_setup()
    _L0_ffn_in = {k: v for k, v in _L0_ffn_all.items() if k in ('router_w', 'w1', 'b1', 'w2', 'b2')}
    del _L0_ffn_all
    return {'x': x, 'L0_conv_w_qkv': _L0_conv_in['w_qkv'], 'L0_conv_b_qkv': _L0_conv_in['b_qkv'], 'L0_conv_w_proj': _L0_conv_in['w_proj'], 'L0_conv_b_proj': _L0_conv_in['b_proj'], 'L0_ffn_router_w': _L0_ffn_in['router_w'], 'L0_ffn_w1': _L0_ffn_in['w1'], 'L0_ffn_b1': _L0_ffn_in['b1'], 'L0_ffn_w2': _L0_ffn_in['w2'], 'L0_ffn_b2': _L0_ffn_in['b2']}

def reference(x, L0_conv_w_qkv, L0_conv_b_qkv, L0_conv_w_proj, L0_conv_b_proj, L0_ffn_router_w, L0_ffn_w1, L0_ffn_b1, L0_ffn_w2, L0_ffn_b2):
    import jax
    import jax.numpy as jnp

    def _L0_conv_ref(x, w_qkv, b_qkv, w_proj, b_proj):
        import jax, jax.numpy as jnp
        import numpy as np
        DIM = 128
        HEADS = 8
        SIZE = 40
        K = 17
        PAD = K // 2
        K2 = K * K

        def _unfold(img, k):
            B, C = (img.shape[0], img.shape[1])
            p = jax.lax.conv_general_dilated_patches(img, (k, k), (1, 1), 'VALID')
            return p.reshape(B, C * k * k, -1)
        B, C, H, W = x.shape
        L = H * W
        c1 = C // HEADS
        scale = c1 ** (-0.5)
        m = jnp.ones((1, 1, H, W), dtype=x.dtype)
        m = jnp.pad(m, ((0, 0), (0, 0), (PAD, PAD), (PAD, PAD)))
        mask_w = _unfold(m, K).transpose(0, 2, 1)
        xt = x.reshape(B, C, L).transpose(0, 2, 1)
        qkv = xt @ w_qkv.T + b_qkv
        q, k, v = jnp.split(qkv, 3, axis=2)
        q = (q * scale).reshape(B, L, HEADS, c1).transpose(0, 2, 1, 3)

        def windows(t):
            img = t.transpose(0, 2, 1).reshape(B, C, H, W)
            img = jnp.pad(img, ((0, 0), (0, 0), (PAD, PAD), (PAD, PAD)))
            flat = _unfold(img, K)
            tw = flat.reshape(B, K2, C, L).transpose(0, 3, 1, 2)
            tw = tw.reshape(B, L, K2, HEADS, c1).transpose(0, 3, 1, 2, 4)
            return tw
        k_w = windows(k)
        v_w = windows(v)
        attn = jnp.einsum('bhnc,bhnlc->bhnl', q, k_w)
        attn = jax.nn.softmax(attn, axis=-1)
        attn = attn * mask_w[:, None]
        out = jnp.einsum('bhnl,bhnlc->bhnc', attn, v_w)
        out = out.transpose(0, 2, 1, 3).reshape(B, L, C)
        out = out @ w_proj.T + b_proj
        out = out.reshape(B, W, H, C).transpose(0, 3, 1, 2)
        return out

    def _L0_ffn_ref(input_embeddings, router_w, w1, b1, w2, b2):
        import jax, jax.numpy as jnp
        import numpy as np
        NUM_EXPERTS = 8
        TOP_K = 2
        B, S, D = (8, 4096, 128)

        def _moe(tokens, router_w, w1, b1, w2, b2):
            N = tokens.shape[0]
            E = router_w.shape[0]
            logits = tokens.astype(jnp.float32) @ router_w.astype(jnp.float32).T
            probs = jax.nn.softmax(logits, axis=-1)
            rw, re = jax.lax.top_k(probs, TOP_K)
            if TOP_K > 1:
                rw = rw / jnp.maximum(rw.sum(-1, keepdims=True), 1e-12)
            rw = rw.astype(tokens.dtype)
            combine = jnp.zeros((N, E), tokens.dtype).at[jnp.arange(N)[:, None], re].set(rw)
            out = tokens
            for e in range(E):
                h = jax.nn.gelu(tokens @ w1[e] + b1[e], approximate=False)
                y = h @ w2[e] + b2[e]
                out = out + combine[:, e:e + 1] * y
            return out
        b, s, d = input_embeddings.shape
        tokens = input_embeddings.reshape(b * s, d)
        return _moe(tokens, router_w, w1, b1, w2, b2).reshape(b, s, d)

    def _gn(v, G=32, eps=1e-05):
        B_, C_, H_, W_ = v.shape
        g = v.reshape(B_, G, C_ // G, H_, W_)
        m = jnp.mean(g, axis=(2, 3, 4), keepdims=True)
        s = jnp.var(g, axis=(2, 3, 4), keepdims=True)
        return ((g - m) / jnp.sqrt(s + eps)).reshape(v.shape)

    def _ln_c(v, eps=1e-06):
        m = jnp.mean(v, axis=1, keepdims=True)
        s = jnp.var(v, axis=1, keepdims=True)
        return (v - m) / jnp.sqrt(s + eps)

    def _ln_t(v, eps=1e-05):
        m = jnp.mean(v, axis=-1, keepdims=True)
        s = jnp.var(v, axis=-1, keepdims=True)
        return (v - m) / jnp.sqrt(s + eps)

    def _to_tokens(v):
        B_, C_, H_, W_ = v.shape
        return v.reshape(B_, C_, H_ * W_).transpose(0, 2, 1)

    def _from_tokens(t, like):
        B_, C_, H_, W_ = like.shape
        return t.transpose(0, 2, 1).reshape(B_, C_, H_, W_)
    x = x + _L0_conv_ref(_ln_c(x), L0_conv_w_qkv, L0_conv_b_qkv, L0_conv_w_proj, L0_conv_b_proj)
    t = _to_tokens(x)
    t = t + _L0_ffn_ref(_ln_t(t), L0_ffn_router_w, L0_ffn_w1, L0_ffn_b1, L0_ffn_w2, L0_ffn_b2)
    x = _from_tokens(t, x)
    return x

_drawn_inputs = setup_inputs


def setup_inputs(seed=0):
    import zlib

    import numpy as np

    out = dict(_drawn_inputs(seed))
    spreads = {'L0_conv_b_qkv': (0.0, 0.8),
     'L0_conv_b_proj': (0.0, 0.1),
     'L0_ffn_b1': (0.0, 0.326),
     'L0_ffn_b2': (0.0, 0.1)}
    factors = {}
    for name, (base, spread) in spreads.items():
        noise = np.random.default_rng([zlib.crc32(name.encode()), seed]).standard_normal(out[name].shape)
        drawn = base * np.exp(spread * noise) if base else spread * noise
        out[name] = jnp.asarray(drawn.astype(out[name].dtype))
    for name, factor in factors.items():
        out[name] = (out[name] * factor).astype(out[name].dtype)
    return out
```

```python
from contextlib import ExitStack

import numpy as np

import concourse.bass as bass
from concourse import mybir

F32 = mybir.dt.float32
I32 = mybir.dt.int32
ALU = mybir.AluOpType
ACT = mybir.ActivationFunctionType
AX = mybir.AxisListType.X

C = 128
HEADS = 8
HC = C // HEADS
SZ = 40
L = SZ * SZ
K = 17
PAD = K // 2
K2 = K * K
PS = SZ + 2 * PAD
IMG = 3168
SLAB = PS * K
NU = (C - 1 + SLAB + C - 1) // C
SKEW = SLAB + C - 1
GW = K2 // HC + HC // 2 - 0
GW = (C - 1 + K2 - 1) // HC + 1
assert GW == 26 and NU == 9
NEG = -1e30
Q = 400
NQ = L // Q
GROW = (SZ - 1) * PS + SZ
GIMG = GROW + HC
YB = [(0, 14, 0), (14, 27, -1), (27, 40, -2)]
SW, SL = 35, 10
NSL = 10
SC = 32
PW, PL, NPS = 36, 12, 11
PN = PL + PW * SZ + 4
E8 = 8
TT = 100
NT = L // TT


def consts():
    s = np.arange(C)
    co = 97 * s % C
    assert ((K2 * co) % C == s).all()
    base = K2 * co // C
    r, hs = s % HC, s // HC
    w = np.arange(GW)
    y = np.arange(SZ)
    start = HC * w[None] - s[:, None]
    valid = (start >= 0) & (start + HC - 1 <= K2 - 1)
    t = {}
    t["neg"] = np.where(valid, 0.0, NEG)
    l = base[:, None] + np.arange(4)[None]
    dy, dx = l // K - PAD, l % K - PAD
    row = lambda d: (y[None, None] + d[:, :, None] >= 0) & (y[None, None] + d[:, :, None] < SZ)
    rm, cm = row(dy), row(dx)
    t["rv"] = rm[:, w // 8, :].transpose(0, 2, 1) & valid[:, None, :]
    t["cm"] = cm
    t["r0"] = rm[:, 0, :]
    t["hot"] = (hs[:, None] == np.arange(8)[None]) & (r[:, None] != 0)
    p = s[:, None, None]
    yy = y[None, :, None]
    t0 = np.zeros(SZ, int)
    for a, b, f in YB:
        t0[a:b] = f
    j = np.arange(NSL)[None, None] + t0[None, :, None]
    t["slot_q"] = (p >= HC * (j - 1) + yy) & (p < HC * j + yy)
    j = np.arange(NPS)[None, None] - 2
    t["slot_o"] = (p >= HC * (j - 1) + yy) & (p < HC * j + yy)
    t["head_o"] = ((p - K * yy) % C) // HC == np.arange(8)[None, None]
    t["ident"] = np.eye(C)
    q = np.arange(C)
    t["unperm"] = (HC * (q % 8) + q // 8)[:, None] == s[None]
    t["perm"] = t["unperm"].T
    t["sel"] = (HC * (q % 8) + HC - 1)[:, None] == np.arange(C + HC - 1)[None]
    e = np.zeros((C, E8, C))
    for i in range(E8):
        e[i, i, :] = 1.0
    t["exp"] = e
    t["iota"] = np.broadcast_to(np.arange(8), (C, 8))
    off, at, parts = 0, {}, []
    for n, a in t.items():
        a = np.asarray(a, np.float32).reshape(C, -1)
        at[n] = (off, a.shape[1])
        off += a.shape[1]
        parts.append(a)
    return at, np.ascontiguousarray(np.concatenate(parts, 1))


CAT, CTAB = consts()


def touched(u, a, b):
    ys = [y for y in range(a, b) if 8 * u - GW <= y + y // HC <= 8 * u + 7]
    return (ys[0], ys[-1] + 1) if ys else None


def program(nc, x_in, wq_t, wk_t, wv_t, wp_t, bq_rot, bq_s, bkv, bproj, rw_t, w1, b1_t, w2, b2, ctab, out):
    with ExitStack() as ctx:
        def sb(name, cols, dt=F32):
            return ctx.enter_context(nc.sbuf_tensor(name, [C, cols], dt))

        def sem(name):
            return ctx.enter_context(nc.semaphore(name))

        def dram(name, n):
            return nc.dram_tensor(name, [n], F32, kind="Internal")

        def v(t, off, *dims, parts=C, p0=0):
            pitch = t[:].ap[0][0]
            return bass.AP(t[:].tensor, p0 * pitch + off, [[pitch, parts]] + [list(d) for d in dims])

        def dv(t, off, *dims):
            return bass.AP(t[:].tensor, off, [list(d) for d in dims])

        con = sb("con", CTAB.shape[1])

        def cv(name, *dims, off=0, parts=C):
            o, n = CAT[name]
            return v(con, o + off, *(dims or [(1, n)]), parts=parts)

        kimg, vimg = sb("kimg", IMG), sb("vimg", IMG)
        xt, xln = sb("xt", L), sb("xln", L)
        qrot, sbd, ebd = sb("qrot", L), sb("sbd", L), sb("ebd", L)
        frot, drot = sb("frot", L), sb("drot", L)
        tok = frot
        uk = [sb(f"uk{i}", SLAB) for i in range(2)]
        uv = [sb(f"uv{i}", SLAB) for i in range(2)]
        sk = [sb(f"sk{i}", NU * C) for i in range(2)]
        sv = [sb(f"sv{i}", NU * C) for i in range(2)]
        kt = sb("kt", NU * C)
        sc = [sb(f"sc{i}", SC * SZ) for i in range(2)]
        ex = [sb(f"ex{i}", GW * SZ) for i in range(2)]
        pm = [sb(f"pm{i}", PN) for i in range(2)]
        mx = [sb(f"mx{i}", GW * SZ) for i in range(2)]
        hotp = [sb(f"hotp{i}", 8 * SZ) for i in range(2)]
        qs = [sb(f"qs{i}", NSL * SZ) for i in range(2)]
        cmx = [sb(f"cmx{i}", 4) for i in range(2)]
        sbx = [sb(f"sbx{i}", SZ) for i in range(2)]
        pmax = sb("pmax", 3 * C)
        cmax = sb("cmax", 3)
        osel, dsel = sb("osel", NPS * SZ), sb("dsel", 8 * SZ)
        gb = [sb(f"gb{i}", GROW) for i in range(2)]
        pr = [sb(f"pr{i}", L) for i in range(2)]
        wq2, wk, wv, wp = sb("wq2", 2 * C), sb("wk", C), sb("wv", C), sb("wp", C)
        wqs = ex[0]
        bqr, bqs, bk2, bp = sb("bqr", SZ), sb("bqs", HC), sb("bk2", 2), sb("bp", 1)
        rw, b1s, b2s = sb("rw", E8), sb("b1s", E8), sb("b2s", C)
        w1s, w2s = sk
        ones = sb("ones", C)
        mean_w = sb("mean_w", C)
        epst = sb("epst", 2)
        hb = [v(sc[0], i * Q, (1, Q)) for i in range(2)]
        hw = [v(sc[1], i * Q, (1, Q)) for i in range(2)]
        lg = drot
        combt = sbd

        ps = ctx.enter_context(nc.psum_tensor("ps", [C, 8 * 512], F32))

        def bank(b, *dims, off=0, parts=C):
            return v(ps, 512 * b + off, *dims, parts=parts)

        kd, vd = dram("kd", C * IMG), dram("vd", C * IMG)
        krd, kld, vrd, vld = (dram(n, C * GIMG) for n in ("krd", "kld", "vrd", "vld"))
        ksl, vsl = dram("ksl", SZ * C * SLAB), dram("vsl", SZ * C * SLAB)
        frd, drd = dram("frd", 2 * C * L), dram("drd", 2 * C * L)

        names = """x_in w_kv w_q w_late consts const_set zero_img zero_buf
            mean_ready centred sq_ready var_ready std_ready rstd_ready normed
            k_ready v_ready k_copied v_copied qr_ready qr_copied bq_scaled wqs_ready
            img_k_out img_v_out shift_k shift_v
            pq_ready kprod kacc sb_copied
            slab_copied kt_ready kt_copied scores_done scores_evac scores_full part_max max_t col_max
            max_bc shifted exps fetched mask_ready q_slots hot masked den_done av_done o_used den_used
            fd_ready eb_red eb_masked eb_perm vprod vacc rot_out nat_in zsum rden att_nat proj_done
            resid logit_ready route comb_ready comb_t comb_copied
            h_ready c_ready gelu_done weighted y_done y_evac y_sum out_sent""".split()
        S = {n: sem(n) for n in names}
        stored = [sem(f"stored{i}") for i in range(2)]
        skewk = [sem(f"skewk{i}") for i in range(2)]
        skewv = [sem(f"skewv{i}") for i in range(2)]
        gload = [sem(f"gload{i}") for i in range(2)]
        block = ctx.enter_context(nc.Block())

        def px(j, o):
            return 2 * j + o

        def half(j, o):
            return j + (o >> 1)

        FULL_LO, FULL_HI = 4, 36

        def steps(eng, fn):
            for o in range(FULL_LO):
                fn(0, o, o)
            with eng.Fori(FULL_LO // 2, FULL_HI // 2) as j:
                for o in range(2):
                    fn(j, o, None)
            for o in range(FULL_HI, SZ + 2):
                fn(0, o, o)

        def on(at, d):
            return at is None or 0 <= at + d < SZ

        def shifted_images(eng, img, right, left, done):
            for r in range(HC):
                eng.dma_start(dv(right, 8 * r * GIMG, (GIMG, 8), (1, GIMG)),
                              dv(img, r * IMG - r, (HC * IMG, 8), (1, GIMG))).then_inc(done, 16)
                if r:
                    at = PAD * 2 * PS + K - r
                    for h0, h1 in ((0, 2), (2, 8)):
                        src = (HC * ((h0 - 2) % 8) + r - 1) * IMG + at
                        eng.dma_start(dv(left, (8 * r + h0) * GIMG, (GIMG, h1 - h0), (1, GIMG)),
                                      dv(img, src, (HC * IMG, h1 - h0), (1, GIMG))).then_inc(done, 16)

        NSHIFT = HC + 2 * (HC - 1)
        ROT = []
        for y in range(SZ):
            if not ROT or K * y // C != K * ROT[-1][0] // C:
                ROT.append([y, y])
            ROT[-1][1] = y + 1

        def load_g(eng, right, left, cc):
            n = 8 * (cc + 1)
            g = gb[cc & 1]
            eng.dma_start(v(g, 0, (1, GROW), parts=n), dv(right, cc, (GIMG, n), (1, GROW))).then_inc(gload[cc & 1], 16)
            if n < C:
                eng.dma_start(v(g, 0, (1, GROW), parts=C - n, p0=n),
                              dv(left, n * GIMG + cc, (GIMG, C - n), (1, GROW))).then_inc(gload[cc & 1], 16)

        def g_loaded(phase, cc):
            count = lambda c: sum(1 if k == HC - 1 else 2 for k in range(c & 1, c + 1, 2))
            return 16 * (phase * count(HC - 2 + (cc & 1)) + count(cc))

        def lgv(i, *dims):
            return v(lg, i * NT * 8, *(dims or [(8, NT), (1, 8)]), parts=TT)

        mm = nc.tensor.matmul

        NROUTE = 25

        @block.sync
        def _(sp):
            sp.wait_ge(S["const_set"], 5)
            for k in range(NQ):
                sp.dma_start(xt[:, k * Q:(k + 1) * Q], x_in[:, k * Q:(k + 1) * Q]).then_inc(S["x_in"], 16)
            sp.dma_start(wk[:], wk_t).then_inc(S["w_kv"], 16)
            sp.dma_start(wv[:], wv_t).then_inc(S["w_kv"], 16)
            sp.dma_start(bk2[:], bkv).then_inc(S["w_kv"], 16)
            sp.dma_start(bp[:], bproj).then_inc(S["w_late"], 16)
            sp.dma_start(wp[:], wp_t).then_inc(S["w_late"], 16)
            sp.dma_start(rw[:], rw_t).then_inc(S["w_late"], 16)
            sp.dma_start(b1s[:], b1_t).then_inc(S["w_late"], 16)
            sp.dma_start(b2s[0:E8, :], b2).then_inc(S["w_late"], 16)

            sp.wait_ge(S["k_copied"], NQ)
            sp.dma_start(dv(kd, 0, (IMG, C), (1, IMG)), kimg[:]).then_inc(S["img_k_out"], 16)

            def store(j, o):
                x = px(j, o)
                sp.wait_ge(S["slab_copied"], 2 * x + 2)
                sp.dma_start(dv(ksl, x * (C * SLAB), (SLAB, C), (1, SLAB)), uk[o & 1][:]).then_inc(stored[o & 1], 16)
                sp.dma_start(dv(vsl, x * (C * SLAB), (SLAB, C), (1, SLAB)), uv[o & 1][:]).then_inc(stored[o & 1], 16)

            def load_k(j, o, at):
                x = px(j, o)
                sp.wait_ge(stored[o & 1], 32 * half(j, o) + 32)
                if at is None or at >= 2:
                    sp.wait_ge(S["kt_ready"], 3 * x - 3)
                sp.dma_start(v(sk[o & 1], 0, (1, SKEW)),
                             dv(ksl, x * (C * SLAB), (SLAB - 1, C), (1, SKEW))).then_inc(skewk[o & 1], 16)

            def load_v(j, o, at):
                x = px(j, o)
                sp.wait_ge(stored[o & 1], 32 * half(j, o) + 32)
                if at is None or at >= 2:
                    sp.wait_ge(S["av_done"], x - 1)
                sp.dma_start(v(sv[o & 1], 0, (1, SKEW)),
                             dv(vsl, x * (C * SLAB), (SLAB - 1, C), (1, SKEW))).then_inc(skewv[o & 1], 16)

            sp.wait_ge(S["zero_buf"], 6)
            store(0, 0)
            store(0, 1)
            load_k(0, 0, 0)
            load_v(0, 0, 0)
            load_k(0, 1, 1)

            sp.wait_ge(S["img_k_out"], 16)
            shifted_images(sp, kd, krd, kld, S["shift_k"])
            sp.wait_ge(S["shift_k"], NSHIFT * 16)
            for cc in range(HC):
                if cc >= 2:
                    sp.wait_ge(S["kprod"], NQ * (cc - 1))
                load_g(sp, krd, kld, cc)
            store(0, 2)
            store(0, 3)
            load_k(0, 2, 2)

            def step(j, o, at):
                if on(at, 4):
                    store(j, o + 4)
                if on(at, 3):
                    load_k(j, o + 3, None if at is None else at + 3)
                if on(at, 1):
                    load_v(j, o + 1, None if at is None else at + 1)

            steps(sp, step)

            sp.wait_ge(S["kt_ready"], 3 * SZ)
            sp.dma_start(v(w1s, 0, (C, E8), (1, C)), w1.rearrange("e d f -> d e f")).then_inc(S["w_late"], 16)
            sp.dma_start(v(w2s, 0, (C, E8), (1, C)), w2.rearrange("e d f -> d e f")).then_inc(S["w_late"], 16)
            for cc in range(HC):
                if cc == 0:
                    sp.wait_ge(S["shift_v"], NSHIFT * 16)
                if cc < 2:
                    sp.wait_ge(S["kprod"], NQ * HC)
                else:
                    sp.wait_ge(S["vprod"], NQ * (cc - 1))
                load_g(sp, vrd, vld, cc)
                if cc == 1:
                    sp.wait_ge(S["fd_ready"], 2 * SZ)
                    for i in range(2):
                        sp.dma_start(dv(frd, i * C * L, (L, C), (1, L)), frot[:]).then_inc(S["rot_out"], 16)
                        sp.dma_start(dv(drd, i * C * L, (L, C), (1, L)), drot[:]).then_inc(S["rot_out"], 16)
                    sp.wait_ge(S["rot_out"], 64)
                    sp.wait_ge(S["scores_full"], SZ)
                    sp.wait_ge(S["q_slots"], SZ)
                    for src, dst in ((frd, sbd), (drd, qrot)):
                        for y0, y1 in ROT:
                            r0 = K * y0 % C
                            sp.dma_start(v(dst, y0 * SZ, (SZ, y1 - y0), (1, SZ)),
                                         dv(src, r0 * L + y0 * SZ, (L, C), (K * L + SZ, y1 - y0), (1, SZ))
                                         ).then_inc(S["nat_in"], 16)

            for k in range(NQ):
                sp.wait_ge(S["y_sum"], k + 1)
                sp.dma_start(out[:, k * Q:(k + 1) * Q], xln[:, k * Q:(k + 1) * Q]).then_inc(S["out_sent"], 16)
            sp.wait_ge(S["out_sent"], 16 * NQ)

        @block.gpsimd
        def _(pool):
            pool.dma_start(con[:], ctab).then_inc(S["consts"], 16)
            nc.gpsimd.memset(kimg[:], 0.0).then_inc(S["zero_img"], 1)
            nc.gpsimd.memset(vimg[:], 0.0).then_inc(S["zero_img"], 1)
            for i in range(2):
                nc.gpsimd.memset(v(sk[i], SKEW, (1, NU * C - SKEW)), 0.0).then_inc(S["zero_buf"], 1)
                nc.gpsimd.memset(v(sv[i], SKEW, (1, NU * C - SKEW)), 0.0).then_inc(S["zero_buf"], 1)
                nc.gpsimd.memset(pm[i][:], 0.0).then_inc(S["zero_buf"], 1)
            pool.wait_ge(S["v_copied"], NQ)
            pool.dma_start(dv(vd, 0, (IMG, C), (1, IMG)), vimg[:]).then_inc(S["img_v_out"], 16)
            pool.wait_ge(S["img_v_out"], 16)
            shifted_images(pool, vd, vrd, vld, S["shift_v"])

            def slots(j, o, at, more=()):
                x = px(j, o)
                for s_, n in more:
                    pool.wait_ge(S[s_], n)
                if at is None or at >= 2:
                    pool.wait_ge(S["scores_done"], 3 * x - 3)
                nc.gpsimd.tensor_tensor(v(qs[o & 1], 0, (NSL, SZ), (1, NSL)), cv("slot_q", (NSL, SZ), (1, NSL)),
                                        v(qrot, x, (SZ, SZ), (0, NSL)), ALU.mult).then_inc(S["q_slots"], 1)

            def fetch(j, o, at):
                x = px(j, o)
                if at is None or at >= 2:
                    pool.wait_ge(S["mask_ready"], 4 * x - 4)
                    pool.wait_ge(S["scores_full"], x - 1)
                nc.gpsimd.tensor_copy(cmx[o & 1][:], v(con, CAT["cm"][0] + x, (SZ, 4))).then_inc(S["fetched"], 1)
                nc.gpsimd.tensor_copy(sbx[o & 1][:], v(sbd, x, (SZ, SZ))).then_inc(S["fetched"], 1)

            def mask_waits(j, o, at):
                x = px(j, o)
                w = [("fetched", 2 * x + 2)]
                return w + [("masked", x - 1)] if at is None or at >= 2 else w

            def mask(j, o, at):
                if at is not None:
                    for s_, n in mask_waits(j, o, at):
                        pool.wait_ge(S[s_], n)
                for m in range(4):
                    n = min(8, GW - 8 * m)
                    nc.gpsimd.tensor_scalar(v(mx[o & 1], 8 * m, (GW, SZ), (1, n)), cv("rv", (GW, SZ), (1, n), off=8 * m),
                                            cmx[o & 1][:, m:m + 1], None, ALU.mult
                                            ).then_inc(S["mask_ready"], 1)

            def pick(j, o, at):
                x = px(j, o)
                pool.wait_ge(S["exps"], x + 1)
                if at is None or at >= 2:
                    pool.wait_ge(S["eb_red"], x - 1)
                nc.gpsimd.tensor_tensor(v(hotp[o & 1], 0, (8, SZ), (1, 8)), v(ex[o & 1], 0, (GW, SZ), (1, 8)),
                                        cv("hot", (0, SZ), (1, 8)), ALU.mult).then_inc(S["hot"], 1)

            pool.wait_ge(S["consts"], 16)
            pool.wait_ge(S["qr_copied"], NQ)
            slots(0, 0, 0)
            slots(0, 1, 1)
            pool.wait_ge(S["sb_copied"], NQ)
            fetch(0, 0, 0)

            def step(j, o, at):
                if on(at, 1):
                    fetch(j, o + 1, None if at is None else at + 1)
                if on(at, 2):
                    slots(j, o + 2, None if at is None else at + 2, mask_waits(j, o, None) if at is None else ())
                if on(at, 0):
                    mask(j, o, at)
                if on(at, -1):
                    pick(j, o - 1, None if at is None else at - 1)

            steps(pool, step)

        def norm_scalar(act, n0, src, dst, eps):
            for k in range(NQ):
                act.wait_ge(S["centred"], n0 + k + 1)
                nc.scalar.activation(dst[:, k * Q:(k + 1) * Q], src[:, k * Q:(k + 1) * Q], ACT.Square
                                     ).then_inc(S["sq_ready"], 1)
            for k in range(NQ):
                act.wait_ge(S["var_ready"], n0 + k + 1)
                nc.scalar.activation(dst[:, k * Q:(k + 1) * Q], bank(4 + k, (1, Q)), ACT.Sqrt,
                                     bias=epst[:, eps:eps + 1]).then_inc(S["std_ready"], 1)

        @block.scalar
        def _(act):
            act.dma_start(wq2[:, 0:C], wq_t).then_inc(S["w_q"], 16)
            act.dma_start(wq2[:, C:2 * C], wq_t).then_inc(S["w_q"], 16)
            act.dma_start(bqr[:], bq_rot).then_inc(S["w_q"], 16)
            act.dma_start(bqs[:], bq_s).then_inc(S["w_q"], 16)
            act.wait_ge(S["const_set"], 4)
            norm_scalar(act, 0, tok, pr[0], 0)
            act.wait_ge(S["w_kv"], 48)
            for dst, b, ready, copied, first, zero in ((kimg, 0, "k_ready", "k_copied", 0, 1), (vimg, 1, "v_ready", "v_copied", 4, 2)):
                act.wait_ge(S["zero_img"], zero)
                for k in range(NQ):
                    act.wait_ge(S[ready], k + 1)
                    nc.scalar.activation(v(dst, (PAD + 10 * k) * PS + PAD, (PS, 10), (1, SZ)),
                                         bank(first + k, (SZ, 10), (1, SZ)), ACT.Identity,
                                         bias=bk2[:, b:b + 1]).then_inc(S[copied], 1)

            def slab(j, o, at):
                x = px(j, o)
                if at is None or at >= 2:
                    act.wait_ge(stored[o & 1], 32 * half(j, o))
                nc.scalar.activation(v(uk[o & 1], 0, (K, PS), (1, K)), v(kimg, x, (PS, PS), (1, K)), ACT.Copy
                                     ).then_inc(S["slab_copied"], 1)
                nc.scalar.activation(v(uv[o & 1], 0, (K, PS), (1, K)), v(vimg, x, (PS, PS), (1, K)), ACT.Copy
                                     ).then_inc(S["slab_copied"], 1)

            def kt_copy(j, o, at, g):
                x = px(j, o)
                if g == 0 and (at is None or at >= 1):
                    act.wait_ge(S["scores_done"], 3 * x)
                act.wait_ge(S["kt_ready"], 3 * x + g + 1)
                n = (4, 4, 1)[g] * C
                nc.scalar.activation(v(kt, 4 * g * C, (1, n)), bank(3 + (g & 1), (1, n)), ACT.Copy
                                     ).then_inc(S["kt_copied"], 1)

            def exps(j, o, at):
                x = px(j, o)
                act.wait_ge(S["shifted"], x + 1)
                if at is None or at >= 2:
                    act.wait_ge(S["masked"], x - 1)
                    act.wait_ge(S["den_done"], x - 1)
                    act.wait_ge(S["hot"], x - 1)
                nc.scalar.activation(v(ex[o & 1], 0, (GW, SZ), (1, GW)), v(sc[o & 1], 0, (SC, SZ), (1, GW)), ACT.Exp
                                     ).then_inc(S["exps"], 1)

            act.wait_ge(S["k_copied"], NQ)
            act.wait_ge(S["v_copied"], NQ)
            slab(0, 0, 0)
            slab(0, 1, 1)
            for k in range(NQ):
                act.wait_ge(S["kacc"], HC)
                nc.scalar.mul(sbd[:, k * Q:(k + 1) * Q], bank(4 + k, (1, Q)), HC ** -0.5).then_inc(S["sb_copied"], 1)
            for x in range(2):
                for g in range(3):
                    kt_copy(0, x, x, g)
            slab(0, 2, 2)
            slab(0, 3, 3)

            def step(j, o, at):
                if on(at, 4):
                    slab(j, o + 4, None if at is None else at + 4)
                if on(at, 2):
                    kt_copy(j, o + 2, None if at is None else at + 2, 0)
                    kt_copy(j, o + 2, None if at is None else at + 2, 1)
                if on(at, 0):
                    exps(j, o, at)
                if on(at, 2):
                    kt_copy(j, o + 2, None if at is None else at + 2, 2)

            steps(act, step)

            norm_scalar(act, NQ, tok, pr[0], 1)
            act.wait_ge(S["route"], 2)
            nc.scalar.activation(lgv(1), lgv(1), ACT.Exp).then_inc(S["comb_ready"], 1)
            for k in range(NQ):
                act.wait_ge(S["comb_t"], k + 1)
                nc.scalar.activation(v(combt, k * Q, (1, Q), parts=E8), bank(4 + k, (1, Q), parts=E8), ACT.Copy
                                     ).then_inc(S["comb_copied"], 1)

            def gelu(k, e, at):
                t = E8 * k + e
                act.wait_ge(S["h_ready"], t + 1)
                if at or e >= 2:
                    act.wait_ge(S["weighted"], t - 1)
                nc.scalar.activation(hb[e & 1], bank(e & 1, (1, Q)), ACT.Gelu, bias=b1s[:, e:e + 1]
                                     ).then_inc(S["gelu_done"], 1)

            for e in range(E8):
                gelu(0, e, 0)
            with act.Fori(1, NQ) as k:
                for e in range(E8):
                    gelu(k, e, 1)

        def norm_tensor(pe, n0, src, waits):
            for k in range(NQ):
                for s_, n in waits(k):
                    pe.wait_ge(s_, n)
                mm(bank(k, (1, Q)), mean_w[:], src[:, k * Q:(k + 1) * Q], start=True, stop=True
                   ).then_inc(S["mean_ready"], 1)
            for k in range(NQ):
                pe.wait_ge(S["sq_ready"], n0 + k + 1)
                mm(bank(4 + k, (1, Q)), mean_w[:], pr[0][:, k * Q:(k + 1) * Q], start=True, stop=True
                   ).then_inc(S["var_ready"], 1)

        @block.tensor
        def _(pe):
            pe.wait_ge(S["const_set"], 4)
            norm_tensor(pe, 0, xt, lambda k: [(S["x_in"], 16 * NQ)])
            pe.wait_ge(S["w_kv"], 48)
            for w, first, ready in ((wk, 0, "k_ready"), (wv, 4, "v_ready")):
                for k in range(NQ):
                    pe.wait_ge(S["normed"], k + 1)
                    mm(bank(first + k, (1, Q)), w[:], xln[:, k * Q:(k + 1) * Q], start=True, stop=True
                       ).then_inc(S[ready], 1)
            pe.wait_ge(S["w_q"], 64)
            for y in range(SZ):
                if y % 10 == 0:
                    pe.wait_ge(S["k_copied"], y // 10 + 1)
                rho = K * y % C
                last = mm(bank(y // 10, (1, SZ), off=SZ * (y % 10)), wq2[:, C - rho:2 * C - rho],
                          xln[:, y * SZ:(y + 1) * SZ], start=True, stop=True, skip_group_check=True)
                if y % 10 == 9:
                    last.then_inc(S["qr_ready"], 1)
            pe.wait_ge(S["consts"], 16)
            pe.wait_ge(S["wqs_ready"], 2)
            pe.wait_ge(S["v_copied"], NQ)
            for cc in range(HC + 1):
                for k in range(NQ):
                    if cc < HC:
                        if cc == 0:
                            pe.wait_ge(S["qr_copied"], k + 1)
                        else:
                            pe.wait_ge(S["kprod"], NQ * (cc - 1) + k + 1)
                        w = v(ex[cc // 8], (cc % 8) * C, (1, C))
                        mm(bank(k, (1, Q)), w, xln[:, k * Q:(k + 1) * Q], start=True, stop=True
                           ).then_inc(S["pq_ready"], 1)
                if cc:
                    for k in range(NQ):
                        pe.wait_ge(S["kprod"], NQ * (cc - 1) + k + 1)
                        last = mm(bank(4 + k, (1, Q)), cv("unperm"), pr[(cc - 1) & 1][:, k * Q:(k + 1) * Q],
                                  start=(cc == 1), stop=(cc == HC), skip_group_check=True)
                    last.then_inc(S["kacc"], 1)

            def transposes(j, o, at, g):
                x = px(j, o)
                if g == 0:
                    pe.wait_ge(skewk[o & 1], 16 * half(j, o) + 16)
                    if at is None or at >= 1:
                        pe.wait_ge(S["kt_copied"], 3 * x)
                if g == 1:
                    if at is None or at >= 1:
                        pe.wait_ge(S["kt_copied"], 3 * x - 1)
                    if at is None or at >= 2:
                        pe.wait_ge(S["col_max"], x - 1)
                if g == 2:
                    pe.wait_ge(S["kt_copied"], 3 * x + 1)
                for i in range((4, 4, 1)[g]):
                    last = nc.tensor.transpose(bank(3 + (g & 1), (1, C), off=i * C),
                                               v(sk[o & 1], (4 * g + i) * C, (1, C)), cv("ident"))
                last.then_inc(S["kt_ready"], 1)

            def scores(j, o, at):
                x = px(j, o)
                pe.wait_ge(S["kt_copied"], 3 * x + 3)
                pe.wait_ge(S["q_slots"], x + 1)
                for b, (y0, y1, t0) in enumerate(YB):
                    if at is None or at >= 1:
                        pe.wait_ge(S["scores_evac"], 3 * x - 2 + b)
                    parts = [(u, *touched(u, y0, y1)) for u in range(NU) if touched(u, y0, y1)]
                    for n, (u, a, z) in enumerate(parts):
                        at0 = SL + SW * (a - y0) + 8 * u + t0 - 1 - a
                        last = mm(bank(b, (SW - 1, z - a), (1, NSL), off=at0), v(kt, u * C, (1, C)),
                                  v(qs[o & 1], a * NSL, (NSL, z - a), (1, NSL)),
                                  start=(n == 0), stop=(n == len(parts) - 1), skip_group_check=True)
                    last.then_inc(S["scores_done"], 1)

            def max_t(j, o, at):
                x = px(j, o)
                pe.wait_ge(S["part_max"], x + 1)
                pe.wait_ge(S["kt_copied"], 3 * x + 5 if (at is None or at + 1 < SZ) else 3 * x + 2)
                for i in range(3):
                    last = nc.tensor.transpose(bank(4, (1, C), off=i * C), pmax[:, i * C:(i + 1) * C], cv("ident"))
                last.then_inc(S["max_t"], 1)

            def max_bc(j, o, at):
                x = px(j, o)
                pe.wait_ge(S["col_max"], x + 1)
                if at is None or at >= 1:
                    pe.wait_ge(S["shifted"], x)
                for i, n in enumerate((C, C, 64)):
                    last = mm(bank(5, (1, n), off=i * C), v(cmax, i, (0, C), parts=n),
                              cv("ident", (1, n), parts=n), start=True, stop=True, skip_group_check=True)
                last.then_inc(S["max_bc"], 1)

            def sums(j, o, at):
                x = px(j, o)
                pe.wait_ge(S["exps"], x + 1)
                if at is None or at >= 1:
                    pe.wait_ge(S["den_used"], x)
                for m in range(4):
                    n = min(8, GW - 8 * m)
                    last = mm(bank(6, (8, SZ), (1, n)), ones[:], v(ex[o & 1], 8 * m, (GW, SZ), (1, n)),
                              start=(m == 0), stop=(m == 3), skip_group_check=True)
                last.then_inc(S["den_done"], 1)

            def products(j, o, at):
                x = px(j, o)
                pe.wait_ge(S["masked"], x + 1)
                pe.wait_ge(skewv[o & 1], 16 * half(j, o) + 16)
                if at is None or at >= 1:
                    pe.wait_ge(S["o_used"], x)
                for u in range(NU):
                    a, z = touched(u, 0, SZ)
                    at0 = PL + PW * a + 8 * u - 3 - a
                    last = mm(bank(7, (1, NPS * (z - a)), off=NPS * a), v(sv[o & 1], u * C, (1, C)),
                              v(pm[o & 1], at0, (PW - 1, z - a), (1, NPS)),
                              start=(u == 0), stop=(u == NU - 1), skip_group_check=True)
                last.then_inc(S["av_done"], 1)

            pe.wait_ge(S["sb_copied"], NQ)
            for g in range(3):
                transposes(0, 0, 0, g)
            scores(0, 0, 0)
            for g in range(3):
                transposes(0, 1, 1, g)

            def step(j, o, at):
                if on(at, 0):
                    max_t(j, o, at)
                if on(at, 1):
                    scores(j, o + 1, None if at is None else at + 1)
                if on(at, 0):
                    max_bc(j, o, at)
                if on(at, 2):
                    transposes(j, o + 2, None if at is None else at + 2, 0)
                    transposes(j, o + 2, None if at is None else at + 2, 1)
                if on(at, -1):
                    sums(j, o - 1, None if at is None else at - 1)
                if on(at, 2):
                    transposes(j, o + 2, None if at is None else at + 2, 2)
                if on(at, -1):
                    products(j, o - 1, None if at is None else at - 1)

            steps(pe, step)

            pe.wait_ge(S["eb_masked"], 1)
            pe.wait_ge(S["shifted"], SZ)
            pe.wait_ge(S["scores_evac"], 3 * SZ)
            pe.wait_ge(S["kt_copied"], 3 * SZ)
            for k in range(NQ):
                mm(bank(k, (1, Q)), cv("perm"), ebd[:, k * Q:(k + 1) * Q], start=True, stop=True
                   ).then_inc(S["eb_perm"], 1)
            pe.wait_ge(S["fd_ready"], 2 * SZ)
            for cc in range(HC):
                for k in range(NQ):
                    pe.wait_ge(S["vprod"], NQ * cc + k + 1)
                    last = mm(bank(4 + k, (1, Q)), cv("sel", (1, C), off=HC - 1 - cc),
                              pr[cc & 1][:, k * Q:(k + 1) * Q], start=(cc == 0), stop=(cc == HC - 1),
                              skip_group_check=True)
                last.then_inc(S["vacc"], 1)

            pe.wait_ge(S["w_late"], 16 * 7)
            for k in range(NQ):
                pe.wait_ge(S["att_nat"], k + 1)
                mm(bank(k, (1, Q)), wp[:], frot[:, k * Q:(k + 1) * Q], start=True, stop=True
                   ).then_inc(S["proj_done"], 1)
            norm_tensor(pe, NQ, xt, lambda k: [(S["resid"], k + 1)])
            for t in range(NT):
                pe.wait_ge(S["normed"], NQ + t // 4 + 1)
                last = mm(bank(0, (1, 8), off=8 * t, parts=TT), xln[:, t * TT:(t + 1) * TT], rw[:],
                          start=True, stop=True, skip_group_check=True)
            last.then_inc(S["logit_ready"], 1)
            pe.wait_ge(S["route"], NROUTE)
            for t in range(NT):
                last = nc.tensor.transpose(bank(4 + t // 4, (1, TT), off=TT * (t % 4), parts=E8),
                                           v(lg, 8 * t, (1, 8), parts=TT),
                                           cv("ident", (1, TT), parts=TT))
                if t % 4 == 3:
                    last.then_inc(S["comb_t"], 1)
            pe.wait_ge(S["comb_copied"], NQ)

            def expert(k, e, at):
                t = E8 * k + e
                if at or e >= 2:
                    pe.wait_ge(S["gelu_done"], t - 1)
                mm(bank(e & 1, (1, Q)), v(w1s, e * C, (1, C)), v(xln, k * Q, (1, Q)), start=True, stop=True
                   ).then_inc(S["h_ready"], 1)
                if at or e >= 2:
                    pe.wait_ge(S["weighted"], t - 1)
                mm(bank(2 + (e & 1), (1, Q)), cv("exp", (1, C), off=e * C), v(combt, k * Q, (1, Q)),
                   start=True, stop=True).then_inc(S["c_ready"], 1)

            def down(k, e, at):
                t = E8 * k + e
                pe.wait_ge(S["weighted"], t + 1)
                if e == 0 and at:
                    pe.wait_ge(S["y_evac"], k)
                mm(bank(4, (1, Q)), v(w2s, e * C, (1, C)), hw[e & 1], start=(e == 0), stop=False,
                   skip_group_check=True).then_inc(S["y_done"], 1)
                if e == E8 - 1:
                    mm(bank(4, (1, Q)), b2s[:], v(combt, k * Q, (1, Q)),
                       start=False, stop=True, skip_group_check=True).then_inc(S["y_done"], 1)

            def chunk(k, at):
                for e in range(E8 + 1):
                    if e < E8:
                        expert(k, e, at)
                    if e:
                        down(k, e - 1, at)

            chunk(0, 0)
            with pe.Fori(1, NQ) as k:
                chunk(k, 1)

        def norm_vector(dve, n0, src, cen, dst):
            for k in range(NQ):
                c = slice(k * Q, (k + 1) * Q)
                dve.wait_ge(S["mean_ready"], n0 + k + 1)
                nc.vector.tensor_tensor(cen[:, c], src[:, c], bank(k, (1, Q)), ALU.subtract).then_inc(S["centred"], 1)
            for k in range(NQ):
                c = slice(k * Q, (k + 1) * Q)
                dve.wait_ge(S["std_ready"], n0 + k + 1)
                nc.vector.reciprocal(pr[1][:, c], pr[0][:, c]).then_inc(S["rstd_ready"], 1)
                dve.wait_ge(S["rstd_ready"], n0 + k + 1)
                nc.vector.tensor_tensor(dst[:, c], cen[:, c], pr[1][:, c], ALU.mult).then_inc(S["normed"], 1)

        @block.vector
        def _(dve):
            tt = nc.vector.tensor_tensor
            nc.vector.memset(mean_w[:], 1.0 / C).then_inc(S["const_set"], 1)
            nc.vector.memset(ones[:], 1.0).then_inc(S["const_set"], 1)
            nc.vector.memset(epst[:, 0:1], 1e-6).then_inc(S["const_set"], 1)
            nc.vector.memset(epst[:, 1:2], 1e-5).then_inc(S["const_set"], 1)
            nc.vector.memset(b2s[:], 0.0).then_inc(S["const_set"], 1)
            nc.vector.memset(pmax[:], 0.0)
            for i in range(2):
                nc.vector.memset(sc[i][:], NEG)
            dve.wait_ge(S["x_in"], 16 * NQ)
            norm_vector(dve, 0, xt, tok, xln)
            dve.wait_ge(S["w_q"], 64)
            nc.vector.tensor_scalar(bqr[:], bqr[:], HC ** -0.5, None, ALU.mult).then_inc(S["bq_scaled"], 1)
            for i in range(2):
                nc.vector.tensor_copy(v(ex[i], 0, (C, 8), (8, HC), (1, 8)),
                                      v(wq2, 8 * i, (1, 8), (0, HC), (HC, 8))).then_inc(S["wqs_ready"], 1)
            dve.wait_ge(S["bq_scaled"], 1)
            for k in range(NQ):
                dve.wait_ge(S["qr_ready"], k + 1)
                nc.vector.scalar_tensor_tensor(v(qrot, k * Q, (SZ, 10), (1, SZ)), bank(k, (SZ, 10), (1, SZ)), HC ** -0.5,
                                               v(bqr, 10 * k, (1, 10), (0, SZ)), ALU.mult, ALU.add
                                               ).then_inc(S["qr_copied"], 1)
            for cc in range(HC):
                dve.wait_ge(gload[cc & 1], g_loaded(0, cc))
                if cc >= 2:
                    dve.wait_ge(S["kacc"], cc - 1)
                for k in range(NQ):
                    dve.wait_ge(S["pq_ready"], NQ * cc + k + 1)
                    nc.vector.scalar_tensor_tensor(v(pr[cc & 1], k * Q, (SZ, 10), (1, SZ)), bank(k, (SZ, 10), (1, SZ)),
                                                   bqs[:, cc:cc + 1], v(gb[cc & 1], 10 * k * PS, (PS, 10), (1, SZ)),
                                                   ALU.add, ALU.mult).then_inc(S["kprod"], 1)

            def boundary_probs(j, o):
                x = px(j, o)
                dve.wait_ge(S["hot"], x + 1)
                nc.vector.tensor_reduce(v(ebd, x, (SZ, SZ)), v(hotp[o & 1], 0, (8, SZ), (1, 8)), AX, ALU.add
                                        ).then_inc(S["eb_red"], 1)

            def evacuate(j, o, at):
                x = px(j, o)
                if at is None or at >= 2:
                    dve.wait_ge(S["exps"], x - 1)
                for b, (y0, y1, _) in enumerate(YB):
                    dve.wait_ge(S["scores_done"], 3 * x + b + 1)
                    n = y1 - y0
                    tt(v(sc[o & 1], SC * y0, (SC, n), (1, GW)), bank(b, (SW, n), (1, GW), off=SL),
                       cv("neg", (0, n), (1, GW)), ALU.add).then_inc(S["scores_evac"], 1)
                dve.wait_ge(S["scores_evac"], 3 * x + 3)
                dve.wait_ge(S["fetched"], 2 * x + 2)
                if on(at, -2):
                    boundary_probs(j, o - 2)
                nc.vector.copy_predicated(v(sc[o & 1], 0, (SC, SZ), (1, 8)),
                                          cv("hot", (0, SZ), (1, 8)).bitcast(I32),
                                          v(sbx[o & 1], 0, (1, SZ), (0, 8))).then_inc(S["scores_full"], 1)
                dve.wait_ge(S["scores_full"], x + 1)
                if at is None or at >= 1:
                    dve.wait_ge(S["max_t"], x)
                nc.vector.tensor_reduce(v(pmax, 0, (8, SZ), (1, 8)), v(sc[o & 1], 0, (SC, SZ), (1, 8), (8, 4)),
                                        AX, ALU.max).then_inc(S["part_max"], 1)

            def column(j, o, at):
                x = px(j, o)
                dve.wait_ge(S["max_t"], x + 1)
                if at is None or at >= 1:
                    dve.wait_ge(S["max_bc"], x)
                nc.vector.tensor_reduce(cmax[:], bank(4, (C, 3), (1, C)), AX, ALU.max).then_inc(S["col_max"], 1)

            def shift(j, o, at):
                x = px(j, o)
                dve.wait_ge(S["max_bc"], x + 1)
                dve.wait_ge(S["scores_full"], x + 1)
                tile = v(sc[o & 1], 0, (SC, SZ), (8, 4), (1, 8))
                tt(tile, tile, bank(5, (8, SZ), (0, 4), (1, 8)), ALU.subtract).then_inc(S["shifted"], 1)

            def weigh(j, o, at):
                x = px(j, o)
                dve.wait_ge(S["exps"], x + 1)
                dve.wait_ge(S["mask_ready"], 4 * x + 4)
                if at is None or at >= 2:
                    dve.wait_ge(S["av_done"], x - 1)
                tt(v(pm[o & 1], PL, (PW, SZ), (1, GW)), v(ex[o & 1], 0, (GW, SZ), (1, GW)),
                   v(mx[o & 1], 0, (GW, SZ), (1, GW)), ALU.mult).then_inc(S["masked"], 1)

            def pick_out(j, o, at):
                x = px(j, o)
                dve.wait_ge(S["av_done"], x + 1)
                if at is None or at >= 1:
                    dve.wait_ge(S["fd_ready"], 2 * x)
                tt(osel[:], bank(7, (1, NPS * SZ)), cv("slot_o"), ALU.mult).then_inc(S["o_used"], 1)
                dve.wait_ge(S["den_done"], x + 1)
                tt(dsel[:], bank(6, (1, 8 * SZ)), cv("head_o"), ALU.mult).then_inc(S["den_used"], 1)
                dve.wait_ge(S["o_used"], x + 1)
                nc.vector.tensor_reduce(v(frot, x, (SZ, SZ)), v(osel, 0, (NPS, SZ), (1, NPS)), AX, ALU.add
                                        ).then_inc(S["fd_ready"], 1)
                dve.wait_ge(S["den_used"], x + 1)
                nc.vector.tensor_reduce(v(drot, x, (SZ, SZ)), v(dsel, 0, (8, SZ), (1, 8)), AX, ALU.add
                                        ).then_inc(S["fd_ready"], 1)

            dve.wait_ge(S["zero_buf"], 6)

            def step(j, o, at):
                if on(at, 0):
                    evacuate(j, o, at)
                if on(at, -1):
                    weigh(j, o - 1, None if at is None else at - 1)
                if on(at, 0):
                    column(j, o, at)
                if on(at, -2):
                    pick_out(j, o - 2, None if at is None else at - 2)
                if on(at, 0):
                    shift(j, o, at)

            steps(dve, step)

            boundary_probs(0, SZ - 2)
            boundary_probs(0, SZ - 1)
            dve.wait_ge(S["eb_red"], SZ)
            tt(v(pr[1], 0, (SZ, SZ), (1, SZ)), cv("r0", (1, SZ), (0, SZ)), cv("cm", (0, SZ), (1, SZ)), ALU.mult
               ).then_inc(S["zsum"], 1)
            dve.wait_ge(S["zsum"], 1)
            tt(ebd[:], ebd[:], pr[1][:], ALU.mult).then_inc(S["eb_masked"], 1)
            dve.wait_ge(S["eb_masked"], 1)
            for cc in range(HC):
                dve.wait_ge(gload[cc & 1], g_loaded(1, cc))
                if cc >= 2:
                    dve.wait_ge(S["vacc"], cc - 1)
                for k in range(NQ):
                    dve.wait_ge(S["eb_perm"], k + 1)
                    tt(v(pr[cc & 1], k * Q, (SZ, 10), (1, SZ)), bank(k, (SZ, 10), (1, SZ)),
                       v(gb[cc & 1], 10 * k * PS, (PS, 10), (1, SZ)), ALU.mult).then_inc(S["vprod"], 1)
            dve.wait_ge(S["nat_in"], 16 * 2 * len(ROT))
            dve.wait_ge(S["vacc"], HC)
            for k in range(NQ):
                c = slice(k * Q, (k + 1) * Q)
                nc.vector.reciprocal(drot[:, c], qrot[:, c]).then_inc(S["rden"], 1)
                tt(sbd[:, c], sbd[:, c], bank(4 + k, (1, Q)), ALU.add).then_inc(S["zsum"], 1)
                dve.wait_ge(S["rden"], k + 1)
                dve.wait_ge(S["zsum"], k + 2)
                tt(frot[:, c], sbd[:, c], drot[:, c], ALU.mult).then_inc(S["att_nat"], 1)
            for k in range(NQ):
                c = slice(k * Q, (k + 1) * Q)
                dve.wait_ge(S["proj_done"], k + 1)
                nc.vector.scalar_tensor_tensor(xt[:, c], bank(k, (1, Q)), bp[:, 0:1], xt[:, c], ALU.add, ALU.add
                                               ).then_inc(S["resid"], 1)
            dve.wait_ge(S["resid"], NQ)
            norm_vector(dve, NQ, xt, tok, xln)

            count = [0]

            def link(ins, last=False):
                count[0] += 1
                ins.then_inc(S["route"], 1)
                if not last:
                    dve.wait_ge(S["route"], count[0])

            col = lambda i, bc=False: v(lg, 11 * NT * 8 + i * NT, (1, NT), *([(0, 8)] if bc else []), parts=TT)
            iota = cv("iota", (0, NT), (1, 8), parts=TT)
            red = lambda o, i, op: nc.vector.tensor_reduce(o, i, AX, op)
            dve.wait_ge(S["logit_ready"], 1)
            lb = bank(0, (8, NT), (1, 8), parts=TT)
            link(red(col(0), lb, ALU.max))
            link(tt(lgv(1), lb, col(0, True), ALU.subtract))
            dve.wait_ge(S["comb_ready"], 1)
            link(red(col(1), lgv(1), ALU.add))
            link(nc.vector.reciprocal(col(2), col(1)))
            link(tt(lgv(2), lgv(1), col(2, True), ALU.mult))
            for n, (p, eq, oh, top) in enumerate(((lgv(2), lgv(3), lgv(4), 3), (lgv(5), lgv(6), lgv(7), 4))):
                link(red(col(top), p, ALU.max))
                link(tt(eq, p, col(top, True), ALU.is_equal))
                link(nc.vector.scalar_tensor_tensor(eq, eq, -8.0, iota, ALU.mult, ALU.add))
                link(red(col(5 + n), eq, ALU.min))
                link(nc.vector.tensor_scalar(col(5 + n), col(5 + n), 8.0, None, ALU.add))
                link(tt(oh, iota, col(5 + n, True), ALU.is_equal))
                if n == 0:
                    link(nc.vector.scalar_tensor_tensor(lgv(5), oh, -2.0, p, ALU.mult, ALU.add))
            link(tt(col(1), col(3), col(4), ALU.add))
            link(tt(lgv(4), lgv(4), col(3, True), ALU.mult))
            link(tt(lgv(7), lgv(7), col(4, True), ALU.mult))
            link(tt(lgv(4), lgv(4), lgv(7), ALU.add))
            link(nc.vector.tensor_scalar(col(1), col(1), 1e-12, None, ALU.max))
            link(nc.vector.reciprocal(col(2), col(1)))
            link(tt(lgv(0), lgv(4), col(2, True), ALU.mult), last=True)
            assert count[0] == NROUTE, count[0]

            def weighted(k, e, at):
                t = E8 * k + e
                dve.wait_ge(S["gelu_done"], t + 1)
                dve.wait_ge(S["c_ready"], t + 1)
                if e >= 2:
                    dve.wait_ge(S["y_done"], (E8 + 1) * k + e - 1)
                elif at:
                    dve.wait_ge(S["y_done"], (E8 + 1) * k)
                tt(hw[e & 1], hb[e & 1], bank(2 + (e & 1), (1, Q)), ALU.mult).then_inc(S["weighted"], 1)

            def finish(k):
                dve.wait_ge(S["y_done"], (E8 + 1) * k + E8 + 1)
                tt(v(tok, k * Q, (1, Q)), v(xt, k * Q, (1, Q)), bank(4, (1, Q)), ALU.add).then_inc(S["y_evac"], 1)
                dve.wait_ge(S["y_evac"], k + 1)
                tt(v(xln, k * Q, (1, Q)), v(xln, k * Q, (1, Q)), v(tok, k * Q, (1, Q)), ALU.add
                   ).then_inc(S["y_sum"], 1)

            for e in range(E8):
                weighted(0, e, 0)
            finish(0)
            with dve.Fori(1, NQ) as k:
                for e in range(E8):
                    weighted(k, e, 1)
                finish(k)


def kernel(x, L0_conv_w_qkv, L0_conv_b_qkv, L0_conv_w_proj, L0_conv_b_proj,
           L0_ffn_router_w, L0_ffn_w1, L0_ffn_b1, L0_ffn_w2, L0_ffn_b2):
    import concourse.bacc as bacc
    from concourse.bass_utils import run_bass_kernel_spmd

    x, wqkv, bqkv = np.asarray(x), np.asarray(L0_conv_w_qkv), np.asarray(L0_conv_b_qkv)
    s = np.arange(C)
    co = 97 * s % C
    rot = (s[:, None] - K * np.arange(SZ)[None]) % C
    q = np.arange(C)
    grp = HC * (q % 8)[:, None] + np.arange(HC)[None]
    t = np.ascontiguousarray
    arrays = {
        "x_in": t(x.reshape(C, L)),
        "wq_t": t(wqkv[0:C].T), "wk_t": t(wqkv[C:2 * C][co].T), "wv_t": t(wqkv[2 * C:3 * C][co].T),
        "wp_t": t(np.asarray(L0_conv_w_proj).T),
        "bq_rot": t(bqkv[0:C][rot]), "bq_s": t(bqkv[0:C][grp]),
        "bkv": t(np.stack([bqkv[C:2 * C][co], bqkv[2 * C:3 * C][co]], 1)),
        "bproj": t(np.asarray(L0_conv_b_proj).reshape(C, 1)),
        "rw_t": t(np.asarray(L0_ffn_router_w).T),
        "w1": t(np.asarray(L0_ffn_w1)), "b1_t": t(np.asarray(L0_ffn_b1).T),
        "w2": t(np.asarray(L0_ffn_w2)), "b2": t(np.asarray(L0_ffn_b2)),
        "ctab": CTAB,
    }
    nc = bacc.Bacc("TRN2", target_bir_lowering=False, num_devices=1)
    args = [nc.dram_tensor(n, list(a.shape), F32, kind="ExternalInput").ap() for n, a in arrays.items()]
    out = nc.dram_tensor("out", [C, L], F32, kind="ExternalOutput").ap()
    program(nc, *args, out)
    got = run_bass_kernel_spmd(nc, [arrays], core_ids=[0]).results[0]["out"]
    return got.reshape(1, C, SZ, SZ)
```

```python
from contextlib import ExitStack

import numpy as np

import concourse.bass as bass
from concourse import mybir

F32 = mybir.dt.float32
I32 = mybir.dt.int32
ALU = mybir.AluOpType
ACT = mybir.ActivationFunctionType
AX = mybir.AxisListType.X

C = 128
HEADS = 8
HC = C // HEADS
SZ = 40
L = SZ * SZ
K = 17
PAD = K // 2
K2 = K * K
PS = SZ + 2 * PAD
IMG = 3168
SLAB = PS * K
NU = (C - 1 + SLAB + C - 1) // C
SKEW = SLAB + C - 1
GW = K2 // HC + HC // 2 - 0
GW = (C - 1 + K2 - 1) // HC + 1
assert GW == 26 and NU == 9
NEG = -1e30
Q = 400
NQ = L // Q
GROW = (SZ - 1) * PS + SZ
GIMG = GROW + HC - 1
GP = GIMG + 2 * HC
YB = [(0, 14, 0), (14, 27, -1), (27, 40, -2)]
SW, SL = 35, 10
NSL = 10
SC = 32
PW, PL, NPS = 34, 8, 9
PN = PL + PW * SZ + 4
E8 = 8
TT = 100
NT = L // TT


def consts():
    s = np.arange(C)
    co = 97 * s % C
    assert ((K2 * co) % C == s).all()
    base = K2 * co // C
    r, hs = s % HC, s // HC
    w = np.arange(GW)
    y = np.arange(SZ)
    start = HC * w[None] - s[:, None]
    valid = (start >= 0) & (start + HC - 1 <= K2 - 1)
    t = {}
    t["neg"] = np.where(valid, 0.0, NEG)
    l = base[:, None] + np.arange(4)[None]
    dy, dx = l // K - PAD, l % K - PAD
    row = lambda d: (y[None, None] + d[:, :, None] >= 0) & (y[None, None] + d[:, :, None] < SZ)
    rm, cm = row(dy), row(dx)
    t["rv"] = rm[:, w // 8, :].transpose(0, 2, 1) & valid[:, None, :]
    t["cm"] = cm
    t["r0"] = rm[:, 0, :]
    t["hot"] = (hs[:, None] == np.arange(8)[None]) & (r[:, None] != 0)
    p = s[:, None, None]
    yy = y[None, :, None]
    t0 = np.zeros(SZ, int)
    for a, b, f in YB:
        t0[a:b] = f
    j = np.arange(NSL)[None, None] + t0[None, :, None]
    t["slot_q"] = (p >= HC * (j - 1) + yy) & (p < HC * j + yy)
    j = np.arange(NPS)[None, None]
    t["slot_o"] = (p >= HC * (j - 1) + yy % HC) & (p < HC * j + yy % HC)
    t["row_of"] = s[:, None] // 8 == np.arange(HC)[None]
    t["head_of"] = s[:, None] % 8 == s[None] // HC
    t["ident"] = np.eye(C)
    q = np.arange(C)
    t["unperm"] = (HC * (q % 8) + q // 8)[:, None] == s[None]
    t["perm"] = t["unperm"].T
    t["sel"] = (HC * (q % 8) + HC - 1)[:, None] == np.arange(C + HC - 1)[None]
    e = np.zeros((C, E8, C))
    for i in range(E8):
        e[i, i, :] = 1.0
    t["exp"] = e
    t["iota"] = np.broadcast_to(np.arange(8), (C, 8))
    off, at, parts = 0, {}, []
    for n, a in t.items():
        a = np.asarray(a, np.float32).reshape(C, -1)
        at[n] = (off, a.shape[1])
        off += a.shape[1]
        parts.append(a)
    return at, np.ascontiguousarray(np.concatenate(parts, 1))


CAT, CTAB = consts()


def touched(u, a, b):
    ys = [y for y in range(a, b) if 8 * u - GW <= y + y // HC <= 8 * u + 7]
    return (ys[0], ys[-1] + 1) if ys else None


def program(nc, x_in, wq_t, wk_t, wv_t, wp_t, bq_rot, bq_s, bkv, bproj, rw_t, w1, b1_t, w2, b2, ctab, out):
    with ExitStack() as ctx:
        def sb(name, cols, dt=F32):
            return ctx.enter_context(nc.sbuf_tensor(name, [C, cols], dt))

        def sem(name):
            return ctx.enter_context(nc.semaphore(name))

        def dram(name, n):
            return nc.dram_tensor(name, [n], F32, kind="Internal")

        def v(t, off, *dims, parts=C, p0=0):
            pitch = t[:].ap[0][0]
            return bass.AP(t[:].tensor, t[:].offset + p0 * pitch + off, [[pitch, parts]] + [list(d) for d in dims])

        def dv(t, off, *dims):
            return bass.AP(t[:].tensor, off, [list(d) for d in dims])

        con = sb("con", CTAB.shape[1])

        def cv(name, *dims, off=0, parts=C):
            o, n = CAT[name]
            return v(con, o + off, *(dims or [(1, n)]), parts=parts)

        kimg, vimg = sb("kimg", IMG), sb("vimg", IMG)
        xt, xln = sb("xt", L), sb("xln", L)
        qrot, sbd, ebd = sb("qrot", L), sb("sbd", L), sb("ebd", L)
        wide = sb("wide", 2 * L)
        frot, rexp = wide[:, 0:L], wide[:, L:2 * L]
        rt = sb("rt", 3 * SZ)
        dsm = [sb(f"dsm{i}", 8 * SZ) for i in range(2)]
        tok = frot
        uk = [sb(f"uk{i}", SLAB) for i in range(2)]
        uv = [sb(f"uv{i}", SLAB) for i in range(2)]
        sk = [sb(f"sk{i}", NU * C) for i in range(2)]
        slabs = sb("slabs", 4 * NU * C + 2 * GROW)
        sv = [slabs[:, i * NU * C:(i + 1) * NU * C] for i in range(2)]
        kt = [slabs[:, (i + 2) * NU * C:(i + 3) * NU * C] for i in range(2)]
        sc = [sb(f"sc{i}", SC * SZ) for i in range(2)]
        ex = [sb(f"ex{i}", GW * SZ) for i in range(2)]
        pm = [sb(f"pm{i}", PN) for i in range(2)]
        hotp = [sb(f"hotp{i}", 8 * SZ) for i in range(2)]
        qs = [sb(f"qs{i}", NSL * SZ) for i in range(2)]
        cmx = [sb(f"cmx{i}", 4) for i in range(2)]
        sbx = [sb(f"sbx{i}", SZ) for i in range(2)]
        pmax = [sb(f"pmax{i}", 3 * C) for i in range(2)]
        cmax = sb("cmax", 3)
        osel = sb("osel", NPS * SZ)
        gb = [slabs[:, 4 * NU * C + i * GROW:4 * NU * C + (i + 1) * GROW] for i in range(2)]
        pr = [sb(f"pr{i}", L) for i in range(2)]
        sh = [v(gb[i], 0, (1, GW * SZ)) for i in range(2)]
        mx = pr
        wq2, wk, wv, wp = sb("wq2", 2 * C), sb("wk", C), sb("wv", C), sb("wp", C)
        qspread = [sv, kt]
        prod = [pr[0], pr[1], ebd, pr[1]]
        gk, gv = [gb[0], gb[1], wide], [kimg, vimg, slabs[:, 2 * NU * C:4 * NU * C], gb[0], gb[1]]
        bqr, bqs, bk2, bp = sb("bqr", SZ), sb("bqs", HC), sb("bk2", 2), sb("bp", 1)
        rw, b1s, b2s = sb("rw", E8), sb("b1s", E8), sb("b2s", C)
        w1s, w2s = sk
        ones = sb("ones", C)
        mean_w = sb("mean_w", C)
        epst = sb("epst", 2)
        stat = sb("stat", 2 * NT)
        hb = [v((kimg, vimg)[e // 4], e % 4 * Q, (1, Q)) for e in range(E8)]
        hw = [v(sc[1], i * Q, (1, Q)) for i in range(2)]
        lg = rexp
        combt = sbd

        ps = ctx.enter_context(nc.psum_tensor("ps", [C, 8 * 512], F32))

        def bank(b, *dims, off=0, parts=C):
            return v(ps, 512 * b + off, *dims, parts=parts)

        krd, kld, vrd, vld = (dram(n, C * GP) for n in ("krd", "kld", "vrd", "vld"))
        ksl, vsl = dram("ksl", SZ * C * SLAB), dram("vsl", SZ * C * SLAB)
        frd = dram("frd", 2 * C * L)
        combd = dram("combd", E8 * L)

        names = """x_in w_kv w_q w_late consts const_set zero_img zero_buf
            mean_ready centred sq_ready var_ready std_ready rstd_ready rstd_spread normed
            k_ready v_ready k_copied v_copied qr_ready qr_copied bq_scaled

            qt_ready qt_copied q_spread
            shift_k shift_v
            pq_ready kprod kpair kacc sb_copied
            slab_copied kt_ready kt_copied scores_done scores_evac scores_full part_max max_t col_max
            max_bc shifted exps boundary_in colmask_in head_sum mask_ready q_slots hot masked den_done av_done o_used
            fd_ready eb_red eb_mask eb_masked eb_perm vprod vacc rot_out nat_in zsum rden rexp_ready r_nat att_nat proj_done
            resid logit_ready route comb_ready comb_t comb_copied
            h_ready comb_out c_ready gelu_done weighted y_done y_evac y_sum out_sent""".split()
        S = {n: sem(n) for n in names}
        stored = [sem(f"stored{i}") for i in range(2)]
        skewk = [sem(f"skewk{i}") for i in range(2)]
        skewv = [sem(f"skewv{i}") for i in range(2)]
        weights_in = [sem(f"weights_in{k}") for k in range(1, NQ)]
        gk_in = [sem(f"gk_in{i}") for i in range(3)]
        gv_in = [sem(f"gv_in{i}") for i in range(5)]
        block = ctx.enter_context(nc.Block())

        def px(j, o):
            return 2 * j + o

        def half(j, o):
            return j + (o >> 1)

        FULL_LO, FULL_HI = 6, 36

        def steps(eng, fn):
            for o in range(FULL_LO):
                fn(0, o, o)
            with eng.Fori(FULL_LO // 2, FULL_HI // 2) as j:
                for o in range(2):
                    fn(j, o, None)
            for o in range(FULL_HI, SZ + 5):
                fn(0, o, o)

        def on(at, d):
            return at is None or 0 <= at + d < SZ

        def shifted_images(eng, img, right, left, done, heads=range(8)):
            for h in heads:
                eng.dma_start(dv(right, h * GP + HC, (8 * GP + 1, HC), (1, GIMG)),
                              v(img, 0, (1, GIMG), parts=HC, p0=HC * h)).then_inc(done, 16)
            at = 2 * PAD * PS + K
            for h in heads:
                eng.dma_start(dv(left, (8 + h) * GP + HC + 1 - (HC - 1), (8 * GP + 1, HC - 1), (1, GIMG + HC - 1)),
                              v(img, at - (HC - 1), (1, GIMG + HC - 1), parts=HC - 1, p0=HC * ((h - 2) % 8))
                              ).then_inc(done, 16)

        NSHIFT = 16
        ROT = []
        for y in range(SZ):
            if not ROT or K * y // C != K * ROT[-1][0] // C:
                ROT.append([y, y])
            ROT[-1][1] = y + 1

        def load_g(eng, right, left, cc, bufs, done):
            n, i = 8 * (cc + 1), cc % len(bufs)
            eng.dma_start(v(bufs[i], 0, (1, GROW), parts=n), dv(right, HC + cc, (GP, n), (1, GROW))).then_inc(done[i], 16)
            if n < C:
                eng.dma_start(v(bufs[i], 0, (1, GROW), parts=C - n, p0=n),
                              dv(left, n * GP + HC + cc, (GP, C - n), (1, GROW))).then_inc(done[i], 16)

        def g_loaded(cc, nbuf):
            return 16 * sum(1 if c == HC - 1 else 2 for c in range(cc % nbuf, cc + 1, nbuf))

        def weight_slab(j, e):
            return v(slabs, 2 * Q * e + Q * j, (1, Q))

        def weight_last(e):
            return v((qrot, ebd)[e // 4], e % 4 * Q, (1, Q))

        def lgv(i, *dims):
            return v(lg, i * NT * 8, *(dims or [(8, NT), (1, 8)]), parts=TT)

        mm = nc.tensor.matmul

        NROUTE = 25

        @block.sync
        def _(sp):
            sp.wait_ge(S["const_set"], 5)
            for k in range(NQ):
                sp.dma_start(xt[:, k * Q:(k + 1) * Q], x_in[:, k * Q:(k + 1) * Q]).then_inc(S["x_in"], 16)
            sp.dma_start(wk[:], wk_t).then_inc(S["w_kv"], 16)
            sp.dma_start(wv[:], wv_t).then_inc(S["w_kv"], 16)
            sp.dma_start(bk2[:], bkv).then_inc(S["w_kv"], 16)
            sp.dma_start(bp[:], bproj).then_inc(S["w_late"], 16)
            sp.dma_start(wp[:], wp_t).then_inc(S["w_late"], 16)
            sp.dma_start(rw[:], rw_t).then_inc(S["w_late"], 16)
            sp.dma_start(b1s[:], b1_t).then_inc(S["w_late"], 16)
            sp.dma_start(b2s[0:E8, :], b2).then_inc(S["w_late"], 16)

            sp.wait_ge(S["k_copied"], NQ)
            shifted_images(sp, kimg, krd, kld, S["shift_k"])
            def store(j, o):
                x = px(j, o)
                sp.wait_ge(S["slab_copied"], 2 * x + 2)
                sp.dma_start(dv(ksl, x * (C * SLAB), (SLAB, C), (1, SLAB)), uk[o & 1][:]).then_inc(stored[o & 1], 16)
                sp.dma_start(dv(vsl, x * (C * SLAB), (SLAB, C), (1, SLAB)), uv[o & 1][:]).then_inc(stored[o & 1], 16)

            def load_k(j, o, at):
                x = px(j, o)
                sp.wait_ge(stored[o & 1], 32 * half(j, o) + 32)
                if at is None or at >= 2:
                    sp.wait_ge(S["kt_ready"], 3 * x - 3)
                sp.dma_start(v(sk[o & 1], 0, (1, SKEW)),
                             dv(ksl, x * (C * SLAB), (SLAB - 1, C), (1, SKEW))).then_inc(skewk[o & 1], 16)

            def load_v(j, o, at):
                x = px(j, o)
                if at is None or at >= 2:
                    sp.wait_ge(S["av_done"], x - 1)
                sp.wait_ge(stored[o & 1], 32 * half(j, o) + 32)
                sp.dma_start(v(sv[o & 1], 0, (1, SKEW)),
                             dv(vsl, x * (C * SLAB), (SLAB - 1, C), (1, SKEW))).then_inc(skewv[o & 1], 16)

            sp.wait_ge(S["shift_k"], NSHIFT * 16)
            for cc in range(HC):
                if cc >= 3:
                    sp.wait_ge(S["kprod"], NQ * (cc - 2))
                load_g(sp, krd, kld, cc, gk, gk_in)
                if cc == 1:
                    store(0, 0)
                    store(0, 1)
                if cc == 3:
                    sp.wait_ge(S["zero_buf"], 6)
                    load_k(0, 0, 0)
                    load_k(0, 1, 1)
                if cc == 9:
                    store(0, 2)
                    store(0, 3)
            load_k(0, 2, 2)

            def step(j, o, at):
                if on(at, 4):
                    store(j, o + 4)
                if on(at, 3):
                    load_k(j, o + 3, None if at is None else at + 3)
                if on(at, -2):
                    load_v(j, o - 2, None if at is None else at - 2)
                if at in (38, 39):
                    sp.wait_ge(S["slab_copied"], 2 * SZ)
                    sp.wait_ge(S["shift_v"], NSHIFT * 16)
                    load_g(sp, vrd, vld, at - 38, gv, gv_in)
                if at == 40:
                    sp.wait_ge(S["scores_done"], 3 * SZ)
                    load_g(sp, vrd, vld, 2, gv, gv_in)
                if at in (42, 43):
                    sp.wait_ge(S["exps"], SZ)
                    load_g(sp, vrd, vld, at - 39, gv, gv_in)
                if at in (1, 2, 3, 4):
                    sp.wait_ge(S["v_copied"], NQ)
                    shifted_images(sp, vimg, vrd, vld, S["shift_v"], range(2 * at - 2, 2 * at))

            steps(sp, step)

            for cc in range(5, HC):
                sp.wait_ge(S["vprod"], NQ * (cc - 4))
                load_g(sp, vrd, vld, cc, gv, gv_in)
                if cc == 12:
                    sp.wait_ge(S["fd_ready"], SZ)
                    for i in range(2):
                        sp.dma_start(dv(frd, i * C * L, (L, C), (1, L)), frot[:]).then_inc(S["rot_out"], 16)
            sp.wait_ge(S["rot_out"], 32)
            sp.wait_ge(S["boundary_in"], SZ)
            for y0, y1 in ROT:
                r0 = K * y0 % C
                sp.dma_start(v(sbd, y0 * SZ, (SZ, y1 - y0), (1, SZ)),
                             dv(frd, r0 * L + y0 * SZ, (L, C), (K * L + SZ, y1 - y0), (1, SZ))
                             ).then_inc(S["nat_in"], 16)
            sp.wait_ge(S["kt_ready"], 3 * SZ)
            sp.dma_start(v(w1s, 0, (C, E8), (1, C)), w1.rearrange("e d f -> d e f")).then_inc(S["w_late"], 16)
            sp.dma_start(v(w2s, 0, (C, E8), (1, C)), w2.rearrange("e d f -> d e f")).then_inc(S["w_late"], 16)

            sp.wait_ge(S["comb_copied"], NQ)
            sp.dma_start(dv(combd, 0, (L, E8), (1, L)), v(combt, 0, (1, L), parts=E8)).then_inc(S["comb_out"], 16)
            sp.wait_ge(S["comb_out"], 16)
            for k in range(1, NQ - 1):
                sp.dma_start(v(slabs, (k - 1) * Q, (2 * Q, E8), (1, Q)),
                             dv(combd, k * Q, (0, C), (L, E8), (1, Q))).then_inc(weights_in[k - 1], 16)
            for i in range(2):
                sp.dma_start(v((qrot, ebd)[i], 0, (Q, 4), (1, Q)),
                             dv(combd, 4 * i * L + (NQ - 1) * Q, (0, C), (L, 4), (1, Q))).then_inc(weights_in[NQ - 2], 16)

            for k in range(NQ):
                sp.wait_ge(S["y_sum"], k + 1)
                sp.dma_start(out[:, k * Q:(k + 1) * Q], xln[:, k * Q:(k + 1) * Q]).then_inc(S["out_sent"], 16)
            sp.wait_ge(S["out_sent"], 16 * NQ)

        @block.gpsimd
        def _(pool):
            nc.gpsimd.memset(kimg[:], 0.0).then_inc(S["zero_img"], 1)
            nc.gpsimd.memset(vimg[:], 0.0).then_inc(S["zero_img"], 1)
            pool.wait_ge(S["x_in"], 16 * NQ)
            pool.dma_start(con[:], ctab).then_inc(S["consts"], 16)
            for i in range(2):
                nc.gpsimd.memset(v(sk[i], SKEW, (1, NU * C - SKEW)), 0.0).then_inc(S["zero_buf"], 1)
                nc.gpsimd.memset(v(sv[i], SKEW, (1, NU * C - SKEW)), 0.0).then_inc(S["zero_buf"], 1)
                nc.gpsimd.memset(pm[i][:], 0.0).then_inc(S["zero_buf"], 1)

            def slots(j, o, at):
                x = px(j, o)
                if at is None or at >= 2:
                    pool.wait_ge(S["scores_done"], 3 * x - 3)
                nc.gpsimd.tensor_tensor(v(qs[o & 1], 0, (NSL, SZ), (1, NSL)), cv("slot_q", (NSL, SZ), (1, NSL)),
                                        v(qrot, x, (SZ, SZ), (0, NSL)), ALU.mult).then_inc(S["q_slots"], 1)

            def fetch_scores(j, o, at):
                x = px(j, o)
                if at is None or at >= 2:
                    pool.wait_ge(S["scores_full"], x - 1)
                nc.gpsimd.tensor_copy(sbx[o & 1][:], v(sbd, x, (SZ, SZ))).then_inc(S["boundary_in"], 1)

            def fetch_mask(j, o, at):
                x = px(j, o)
                if at is None or at >= 2:
                    pool.wait_ge(S["mask_ready"], 4 * x - 4)
                nc.gpsimd.tensor_copy(cmx[o & 1][:], v(con, CAT["cm"][0] + x, (SZ, 4))).then_inc(S["colmask_in"], 1)

            def pick(j, o, at):
                x = px(j, o)
                pool.wait_ge(S["exps"], x + 1)
                if at is None or at >= 2:
                    pool.wait_ge(S["eb_red"], x - 1)
                nc.gpsimd.tensor_tensor(v(hotp[o & 1], 0, (8, SZ), (1, 8)), v(ex[o & 1], 0, (GW, SZ), (1, 8)),
                                        cv("hot", (0, SZ), (1, 8)), ALU.mult).then_inc(S["hot"], 1)

            def sum_heads(j, o, at):
                x = px(j, o)
                d, e = dsm[o & 1], ex[o & 1]
                if at is None or at >= 2:
                    pool.wait_ge(S["den_done"], x - 1)
                nc.gpsimd.tensor_tensor(v(d, 0, (8, SZ), (1, 8)), v(e, 0, (GW, SZ), (1, 8)), v(e, 8, (GW, SZ), (1, 8)),
                                        ALU.add).then_inc(S["head_sum"], 1)
                for m, n in ((2, 8), (3, 2)):
                    pool.wait_ge(S["head_sum"], 3 * x + m - 1)
                    nc.gpsimd.tensor_tensor(v(d, 0, (8, SZ), (1, n)), v(d, 0, (8, SZ), (1, n)),
                                            v(e, 8 * m, (GW, SZ), (1, n)), ALU.add).then_inc(S["head_sum"], 1)

            pool.wait_ge(S["consts"], 16)
            pool.wait_ge(S["qr_copied"], NQ)
            slots(0, 0, 0)
            slots(0, 1, 1)
            pool.wait_ge(S["sb_copied"], NQ)
            fetch_scores(0, 0, 0)

            def step(j, o, at):
                if on(at, 1):
                    fetch_scores(j, o + 1, None if at is None else at + 1)
                if on(at, -1):
                    fetch_mask(j, o - 1, None if at is None else at - 1)
                if on(at, 2):
                    slots(j, o + 2, None if at is None else at + 2)
                if at == SZ - 1:
                    pool.wait_ge(S["q_slots"], SZ)
                    nc.gpsimd.tensor_tensor(v(qrot, 0, (SZ, SZ), (1, SZ)), cv("r0", (1, SZ), (0, SZ)),
                                            cv("cm", (0, SZ), (1, SZ)), ALU.mult).then_inc(S["eb_mask"], 1)
                if on(at, -3):
                    pick(j, o - 3, None if at is None else at - 3)
                    sum_heads(j, o - 3, None if at is None else at - 3)

            steps(pool, step)
            for k in range(NQ):
                pool.wait_ge(S["y_evac"], k + 1)
                nc.gpsimd.tensor_tensor(xln[:, k * Q:(k + 1) * Q], xln[:, k * Q:(k + 1) * Q],
                                        tok[:, k * Q:(k + 1) * Q], ALU.add).then_inc(S["y_sum"], 1)

        def norm_scalar(act, n0, src, dst, eps):
            for k in range(NQ):
                act.wait_ge(S["centred"], n0 + k + 1)
                nc.scalar.activation(dst[:, k * Q:(k + 1) * Q], src[:, k * Q:(k + 1) * Q], ACT.Square
                                     ).then_inc(S["sq_ready"], 1)
            act.wait_ge(S["var_ready"], n0 // NQ + 1)
            nc.scalar.activation(v(stat, 0, (1, NT), parts=TT), bank(0, (1, NT), parts=TT), ACT.Sqrt,
                                 bias=epst[0:TT, eps:eps + 1]).then_inc(S["std_ready"], 1)

        @block.scalar
        def _(act):
            act.dma_start(wq2[:, 0:C], wq_t).then_inc(S["w_q"], 16)
            act.dma_start(wq2[:, C:2 * C], wq_t).then_inc(S["w_q"], 16)
            act.dma_start(bqr[:], bq_rot).then_inc(S["w_q"], 16)
            act.dma_start(bqs[:], bq_s).then_inc(S["w_q"], 16)
            act.wait_ge(S["const_set"], 4)
            norm_scalar(act, 0, tok, pr[0], 0)
            act.wait_ge(S["w_kv"], 48)
            for dst, b, ready, copied, zero in ((kimg, 0, "k_ready", "k_copied", 1), (vimg, 1, "v_ready", "v_copied", 2)):
                if b:
                    for k in range(NQ):
                        act.wait_ge(S["qt_ready"], k + 1)
                        nc.scalar.activation(v(ex[k // 2], (k % 2) * 4 * C, (1, 4 * C), parts=TT),
                                             bank(4 + k, (1, 4 * C), parts=TT), ACT.Copy).then_inc(S["qt_copied"], 1)
                act.wait_ge(S["zero_img"], zero)
                for k in range(NQ):
                    act.wait_ge(S[ready], k + 1)
                    nc.scalar.activation(v(dst, (PAD + 10 * k) * PS + PAD, (PS, 10), (1, SZ)),
                                         bank(k, (SZ, 10), (1, SZ)), ACT.Identity,
                                         bias=bk2[:, b:b + 1]).then_inc(S[copied], 1)

            def slab(j, o, at):
                x = px(j, o)
                if at is None or at >= 2:
                    act.wait_ge(stored[o & 1], 32 * half(j, o))
                nc.scalar.activation(v(uk[o & 1], 0, (K, PS), (1, K)), v(kimg, x, (PS, PS), (1, K)), ACT.Copy
                                     ).then_inc(S["slab_copied"], 1)
                nc.scalar.activation(v(uv[o & 1], 0, (K, PS), (1, K)), v(vimg, x, (PS, PS), (1, K)), ACT.Copy
                                     ).then_inc(S["slab_copied"], 1)

            def kt_copy(j, o, at, g):
                x = px(j, o)
                if g == 0 and (at is None or at >= 2):
                    act.wait_ge(S["scores_done"], 3 * x - 3)
                act.wait_ge(S["kt_ready"], 3 * x + g + 1)
                n = (4, 4, 1)[g] * C
                nc.scalar.activation(v(kt[o & 1], 4 * g * C, (1, n)), bank(3 + (g & 1), (1, n)), ACT.Copy
                                     ).then_inc(S["kt_copied"], 1)

            def exps(j, o, at):
                x = px(j, o)
                act.wait_ge(S["shifted"], x + 1)
                if at is None or at >= 2:
                    act.wait_ge(S["masked"], x - 1)
                    act.wait_ge(S["head_sum"], 3 * x - 3)
                    act.wait_ge(S["hot"], x - 1)
                nc.scalar.activation(ex[o & 1][:], sh[o & 1], ACT.Exp
                                     ).then_inc(S["exps"], 1)

            def mask(j, o, at):
                x = px(j, o)
                act.wait_ge(S["colmask_in"], x + 1)
                act.wait_ge(S["consts"], 16)
                if at is None or at >= 2:
                    act.wait_ge(S["masked"], x - 1)
                for m in range(4):
                    n = min(8, GW - 8 * m)
                    nc.scalar.activation(v(mx[o & 1], 8 * m, (GW, SZ), (1, n)), cv("rv", (GW, SZ), (1, n), off=8 * m),
                                         ACT.Copy, scale=cmx[o & 1][:, m:m + 1]).then_inc(S["mask_ready"], 1)

            act.wait_ge(S["k_copied"], NQ)
            act.wait_ge(S["v_copied"], NQ)
            act.wait_ge(S["qt_copied"], NQ)
            for cc in range(HC):
                if cc >= 2:
                    act.wait_ge(S["pq_ready"], NQ * (cc - 1))
                if cc == 2:
                    slab(0, 0, 0)
                    slab(0, 1, 1)
                if cc == 8:
                    slab(0, 2, 2)
                    slab(0, 3, 3)
                for i in range(2):
                    nc.scalar.activation(v(qspread[cc & 1][i], 0, (C, 8), (8, HC), (1, 8), parts=TT),
                                         v(ex[i], cc, (C, 8), (0, HC), (HC, 8), parts=TT), ACT.Copy
                                         ).then_inc(S["q_spread"], 1)
            kt_copy(0, 0, 0, 0)
            for k in range(NQ):
                act.wait_ge(S["kacc"], HC // 2)
                if k in (1, 2):
                    kt_copy(0, 0, 0, k)
                nc.scalar.mul(sbd[:, k * Q:(k + 1) * Q], bank(4 + k, (1, Q)), HC ** -0.5).then_inc(S["sb_copied"], 1)
            for g in range(3):
                kt_copy(0, 1, 1, g)

            def step(j, o, at):
                if on(at, 4):
                    slab(j, o + 4, None if at is None else at + 4)
                if on(at, 2):
                    kt_copy(j, o + 2, None if at is None else at + 2, 0)
                    kt_copy(j, o + 2, None if at is None else at + 2, 1)
                if on(at, -2):
                    exps(j, o - 2, None if at is None else at - 2)
                if on(at, 2):
                    kt_copy(j, o + 2, None if at is None else at + 2, 2)
                if on(at, -2):
                    mask(j, o - 2, None if at is None else at - 2)

            steps(act, step)

            nc.scalar.activation(stat[0:1, 0:1], epst[0:1, 1:2], ACT.Sqrt)
            norm_scalar(act, NQ, tok, pr[0], 1)
            act.wait_ge(S["route"], 2)
            nc.scalar.activation(lgv(1), lgv(1), ACT.Exp).then_inc(S["comb_ready"], 1)
            def gelu(k, e, at):
                t = E8 * k + e
                act.wait_ge(S["h_ready"], t + 1)
                if at:
                    act.wait_ge(S["weighted"], t - (E8 - 1))
                nc.scalar.activation(hb[e], bank(e & 3 if at else 4 + e % 4, (1, Q)), ACT.Gelu, bias=b1s[:, e:e + 1]
                                     ).then_inc(S["gelu_done"], 1)

            for e in range(E8):
                gelu(0, e, 0)
            for k in range(NQ):
                act.wait_ge(S["comb_t"], k + 1)
                nc.scalar.activation(v(combt, k * Q, (1, Q), parts=E8), bank(4 + k, (1, Q), parts=E8), ACT.Copy
                                     ).then_inc(S["comb_copied"], 1)
            with act.Fori(1, NQ) as k:
                for e in range(E8):
                    gelu(k, e, 1)

        def norm_tensor(pe, n0, src, waits):
            for k in range(NQ):
                for s_, n in waits(k):
                    pe.wait_ge(s_, n)
                mm(bank(k, (1, Q)), mean_w[:], src[:, k * Q:(k + 1) * Q], start=True, stop=True
                   ).then_inc(S["mean_ready"], 1)
            pe.wait_ge(S["centred"], n0 + NQ)
            if n0 == 0:
                pe.wait_ge(S["consts"], 16)
            for t in range(NT):
                pe.wait_ge(S["sq_ready"], n0 + t * TT // Q + 1)
                last = mm(bank(0, (1, 1), off=t, parts=TT), pr[0][:, t * TT:(t + 1) * TT], mean_w[:, 0:1],
                          start=True, stop=True, skip_group_check=True)
            last.then_inc(S["var_ready"], 1)
            pe.wait_ge(S["rstd_ready"], n0 // NQ + 1)
            for t in range(NT):
                last = nc.tensor.transpose(bank(4 + t * TT // Q, (1, TT), off=t * TT % Q), v(stat, NT + t, (0, C), parts=TT),
                                           cv("ident", (1, TT), parts=TT))
                if (t + 1) * TT % Q == 0:
                    last.then_inc(S["rstd_spread"], 1)

        @block.tensor
        def _(pe):
            pe.wait_ge(S["const_set"], 4)
            norm_tensor(pe, 0, xt, lambda k: [(S["x_in"], 16 * NQ)])
            pe.wait_ge(S["w_kv"], 48)
            for k in range(NQ):
                pe.wait_ge(S["normed"], k + 1)
                mm(bank(k, (1, Q)), wk[:], xln[:, k * Q:(k + 1) * Q], start=True, stop=True).then_inc(S["k_ready"], 1)
            pe.wait_ge(S["w_q"], 64)
            for t in range(NT):
                last = mm(bank(4 + t // 4, (1, C), off=C * (t % 4), parts=TT), xln[:, t * TT:(t + 1) * TT], wq2[:, 0:C],
                          start=True, stop=True, skip_group_check=True)
                if t % 4 == 3:
                    last.then_inc(S["qt_ready"], 1)
            for k in range(NQ):
                pe.wait_ge(S["k_copied"], k + 1)
                mm(bank(k, (1, Q)), wv[:], xln[:, k * Q:(k + 1) * Q], start=True, stop=True).then_inc(S["v_ready"], 1)
            for y in range(SZ):
                if y % 10 == 0:
                    pe.wait_ge(S["qt_copied"], y // 10 + 1)
                rho = K * y % C
                last = mm(bank(4 + y // 10, (1, SZ), off=SZ * (y % 10)), wq2[:, C - rho:2 * C - rho],
                          xln[:, y * SZ:(y + 1) * SZ], start=True, stop=True, skip_group_check=True)
                if y % 10 == 9:
                    last.then_inc(S["qr_ready"], 1)
            def transposes(j, o, at, g):
                x = px(j, o)
                if g == 0:
                    pe.wait_ge(skewk[o & 1], 16 * half(j, o) + 16)
                    if at is None or at >= 1:
                        pe.wait_ge(S["kt_copied"], 3 * x)
                if g == 1:
                    if at == 0:
                        pe.wait_ge(S["sb_copied"], 1)
                    if at is None or at >= 1:
                        pe.wait_ge(S["kt_copied"], 3 * x - 1)
                    if at is None or at >= 4:
                        pe.wait_ge(S["col_max"], x - 3)
                if g == 2:
                    pe.wait_ge(S["kt_copied"], 3 * x + 1)
                for i in range((4, 4, 1)[g]):
                    last = nc.tensor.transpose(bank(3 + (g & 1), (1, C), off=i * C),
                                               v(sk[o & 1], (4 * g + i) * C, (1, C)), cv("ident"))
                last.then_inc(S["kt_ready"], 1)

            for cc in range(HC + 2):
                for k in range(NQ):
                    if cc < HC:
                        if cc == 0:
                            pe.wait_ge(S["v_copied"], k + 1)
                        else:
                            pe.wait_ge(S["kprod"], NQ * (cc - 1) + k + 1)
                        pe.wait_ge(S["q_spread"], 2 * cc + k // 2 + 1)
                        for i in range(4):
                            t = 4 * k + i
                            last = nc.tensor.transpose(bank(k, (1, TT), off=TT * i),
                                                       v(qspread[cc & 1][t // 8], (t % 8) * C, (1, C), parts=TT),
                                                       cv("ident", (1, TT), parts=TT))
                        last.then_inc(S["pq_ready"], 1)
                if cc >= 2:
                    pair = cc // 2 - 1
                    pe.wait_ge(S["kpair"], pair + 1)
                    for k in (0, 1) if cc % 2 == 0 else (2, 3):
                        if pair == 0:
                            pe.wait_ge(S["qr_copied"], k + 1)
                        last = mm(bank(4 + k, (1, Q)), cv("unperm"), prod[2 * pair & 3][:, k * Q:(k + 1) * Q],
                                  start=(pair == 0), stop=(2 * pair == HC - 2), skip_group_check=True)
                    if cc & 1:
                        last.then_inc(S["kacc"], 1)
                if cc == HC - 1:
                    pe.wait_ge(S["kprod"], NQ * HC)
                    transposes(0, 0, 0, 0)

            def scores(j, o, at, banks):
                x = px(j, o)
                if banks[0] == 0:
                    pe.wait_ge(S["kt_copied"], 3 * x + 3)
                    pe.wait_ge(S["q_slots"], x + 1)
                for b in banks:
                    y0, y1, t0 = YB[b]
                    if at is None or at >= 1:
                        pe.wait_ge(S["scores_evac"], 3 * x - 2 + b)
                    parts = [(u, *touched(u, y0, y1)) for u in range(NU) if touched(u, y0, y1)]
                    for n, (u, a, z) in enumerate(parts):
                        at0 = SL + SW * (a - y0) + 8 * u + t0 - 1 - a
                        last = mm(bank(b, (SW - 1, z - a), (1, NSL), off=at0), v(kt[o & 1], u * C, (1, C)),
                                  v(qs[o & 1], a * NSL, (NSL, z - a), (1, NSL)),
                                  start=(n == 0), stop=(n == len(parts) - 1), skip_group_check=True)
                    last.then_inc(S["scores_done"], 1)

            def max_t(j, o, at):
                x = px(j, o)
                pe.wait_ge(S["part_max"], x + 1)
                pe.wait_ge(S["kt_copied"], 3 * x + 11 if (at is None or at + 3 < SZ) else 3 * SZ - 1)
                for i in range(3):
                    last = nc.tensor.transpose(bank(4, (1, C), off=i * C), pmax[o & 1][:, i * C:(i + 1) * C], cv("ident"))
                last.then_inc(S["max_t"], 1)

            def max_bc(j, o, at):
                x = px(j, o)
                pe.wait_ge(S["col_max"], x + 1)
                if at is None or at >= 1:
                    pe.wait_ge(S["shifted"], x)
                for i, n in enumerate((C, C, 64)):
                    last = nc.tensor.transpose(bank(5, (1, n), off=i * C), v(cmax, i, (0, C), parts=n),
                                               cv("ident", (1, n), parts=n))
                last.then_inc(S["max_bc"], 1)

            def sums(j, o, at):
                x = px(j, o)
                pe.wait_ge(S["head_sum"], 3 * x + 3)
                for i, n in enumerate((C, C, 64)):
                    last = mm(v(ps, 512 * 6 + 3 * x + i, (1, 1), parts=n), v(dsm[o & 1], i * C, (1, n)), ones[:, 0:1],
                              start=True, stop=True, skip_group_check=True)
                last.then_inc(S["den_done"], 1)

            def products(j, o, at):
                x = px(j, o)
                pe.wait_ge(S["masked"], x + 1)
                pe.wait_ge(skewv[o & 1], 16 * half(j, o) + 16)
                if at is None or at >= 1:
                    pe.wait_ge(S["o_used"], x)
                for u in range(NU):
                    a, z = touched(u, 0, SZ)
                    at0 = PL + PW * a + 8 * u - 1 - a
                    last = mm(bank(7, (1, NPS * (z - a)), off=NPS * a), v(sv[o & 1], u * C, (1, C)),
                              v(pm[o & 1], at0, (PW - 1, z - a), (1, NPS)),
                              start=(u == 0), stop=(u == NU - 1), skip_group_check=True)
                last.then_inc(S["av_done"], 1)

            for g in (1, 2):
                transposes(0, 0, 0, g)
            scores(0, 0, 0, range(3))
            pe.wait_ge(S["sb_copied"], NQ)
            for g in range(3):
                transposes(0, 1, 1, g)

            def step(j, o, at):
                if on(at, 2):
                    transposes(j, o + 2, None if at is None else at + 2, 0)
                    transposes(j, o + 2, None if at is None else at + 2, 1)
                if on(at, -4):
                    sums(j, o - 4, None if at is None else at - 4)
                if on(at, 1):
                    scores(j, o + 1, None if at is None else at + 1, (0,))
                if on(at, 2):
                    transposes(j, o + 2, None if at is None else at + 2, 2)
                if on(at, -1):
                    max_t(j, o - 1, None if at is None else at - 1)
                if on(at, 1):
                    scores(j, o + 1, None if at is None else at + 1, (1, 2))
                if on(at, -1):
                    max_bc(j, o - 1, None if at is None else at - 1)
                if on(at, -4):
                    products(j, o - 4, None if at is None else at - 4)

            steps(pe, step)

            pe.wait_ge(S["shifted"], SZ)
            pe.wait_ge(S["scores_evac"], 3 * SZ)
            pe.wait_ge(S["kt_copied"], 3 * SZ)
            for k in range(NQ):
                pe.wait_ge(S["eb_masked"], k + 1)
                mm(bank(k, (1, Q)), cv("perm"), ebd[:, k * Q:(k + 1) * Q], start=True, stop=True
                   ).then_inc(S["eb_perm"], 1)
            pe.wait_ge(S["fd_ready"], SZ)
            pe.wait_ge(S["rden"], 2)
            for cc in range(HC):
                for k in range(NQ):
                    pe.wait_ge(S["vprod"], NQ * cc + k + 1)
                    last = mm(bank(4 + k, (1, Q)), cv("sel", (1, C), off=HC - 1 - cc),
                              pr[cc & 1][:, k * Q:(k + 1) * Q], start=(cc == 0), stop=(cc == HC - 1),
                              skip_group_check=True)
                last.then_inc(S["vacc"], 1)

            pe.wait_ge(S["vprod"], NQ * HC)
            for k in range(NQ):
                pe.wait_ge(S["rexp_ready"], 3)
                mm(bank(k, (1, Q)), cv("head_of"), rexp[:, k * Q:(k + 1) * Q], start=True, stop=True
                   ).then_inc(S["r_nat"], 1)
            pe.wait_ge(S["w_late"], 16 * 7)
            for k in range(NQ):
                pe.wait_ge(S["att_nat"], k + 1)
                mm(bank(k, (1, Q)), wp[:], frot[:, k * Q:(k + 1) * Q], start=True, stop=True
                   ).then_inc(S["proj_done"], 1)
            norm_tensor(pe, NQ, xt, lambda k: [(S["resid"], k + 1)])
            for t in range(NT):
                pe.wait_ge(S["normed"], NQ + t // 4 + 1)
                last = mm(bank(0, (1, 8), off=8 * t, parts=TT), xln[:, t * TT:(t + 1) * TT], rw[:],
                          start=True, stop=True, skip_group_check=True)
            last.then_inc(S["logit_ready"], 1)

            def up(k, e, at):
                t = E8 * k + e
                if at or e >= 4:
                    pe.wait_ge(S["gelu_done"], t - 3)
                mm(bank(e & 3 if at else 4 + e % 4, (1, Q)), v(w1s, e * C, (1, C)), v(xln, k * Q, (1, Q)),
                   start=True, stop=True).then_inc(S["h_ready"], 1)

            def spread(e):
                if e >= 2:
                    pe.wait_ge(S["weighted"], e - 1)
                for i in range(4):
                    last = nc.tensor.transpose(bank(2 + (e & 1), (1, TT), off=TT * i),
                                               v(lg, E8 * i + e, (0, C), parts=TT),
                                               cv("ident", (1, TT), parts=TT))
                last.then_inc(S["c_ready"], 1)

            def down(k, e, at):
                t = E8 * k + e
                if e == 0:
                    if at:
                        pe.wait_ge(S["y_evac"], k)
                    mm(bank(4, (1, Q)), b2s[:], v(combt, k * Q, (1, Q)),
                       start=True, stop=False, skip_group_check=True).then_inc(S["y_done"], 1)
                pe.wait_ge(S["weighted"], t + 1)
                mm(bank(4, (1, Q)), v(w2s, e * C, (1, C)), hw[e & 1], start=False, stop=(e == E8 - 1),
                   skip_group_check=True).then_inc(S["y_done"], 1)

            for e in range(E8):
                up(0, e, 0)
            pe.wait_ge(S["route"], NROUTE)
            spread(0)
            spread(1)
            for t in range(NT):
                if t == 0:
                    pe.wait_ge(S["gelu_done"], E8)
                last = nc.tensor.transpose(bank(4 + t // 4, (1, TT), off=TT * (t % 4), parts=E8),
                                           v(lg, 8 * t, (1, 8), parts=TT),
                                           cv("ident", (1, TT), parts=TT))
                if t % 4 == 3:
                    last.then_inc(S["comb_t"], 1)
            pe.wait_ge(S["comb_copied"], NQ)
            for e in range(E8):
                if 1 <= e < E8 - 1:
                    spread(e + 1)
                if e >= E8 - 2:
                    up(1, e - (E8 - 2), 1)
                down(0, e, 0)

            def chunk(k, last):
                for e in range(E8):
                    if e < E8 - 2:
                        up(k, e + 2, 1)
                    elif not last:
                        up(k + 1, e - (E8 - 2), 1)
                    down(k, e, 1)

            with pe.Fori(1, NQ - 1) as k:
                chunk(k, False)
            chunk(NQ - 1, True)

        def norm_vector(dve, n0, src, cen, dst):
            for k in range(NQ):
                c = slice(k * Q, (k + 1) * Q)
                dve.wait_ge(S["mean_ready"], n0 + k + 1)
                nc.vector.tensor_tensor(cen[:, c], src[:, c], bank(k, (1, Q)), ALU.subtract).then_inc(S["centred"], 1)
            dve.wait_ge(S["std_ready"], n0 // NQ + 1)
            nc.vector.reciprocal(v(stat, NT, (1, NT), parts=TT), v(stat, 0, (1, NT), parts=TT)).then_inc(S["rstd_ready"], 1)
            for k in range(NQ):
                c = slice(k * Q, (k + 1) * Q)
                dve.wait_ge(S["rstd_spread"], n0 + k + 1)
                nc.vector.tensor_tensor(dst[:, c], cen[:, c], bank(4 + k, (1, Q)), ALU.mult).then_inc(S["normed"], 1)

        @block.vector
        def _(dve):
            tt = nc.vector.tensor_tensor
            nc.vector.memset(mean_w[:], 1.0 / C).then_inc(S["const_set"], 1)
            nc.vector.memset(ones[:], 1.0).then_inc(S["const_set"], 1)
            nc.vector.memset(epst[:, 0:1], 1e-6).then_inc(S["const_set"], 1)
            nc.vector.memset(epst[:, 1:2], 1e-5).then_inc(S["const_set"], 1)
            nc.vector.memset(b2s[:], 0.0).then_inc(S["const_set"], 1)
            for i in range(2):
                nc.vector.memset(sc[i][:], NEG)
                nc.vector.memset(pmax[i][:], 0.0)
            dve.wait_ge(S["x_in"], 16 * NQ)
            norm_vector(dve, 0, xt, tok, xln)
            dve.wait_ge(S["w_q"], 64)
            nc.vector.tensor_scalar(bqr[:], bqr[:], HC ** -0.5, None, ALU.mult).then_inc(S["bq_scaled"], 1)
            dve.wait_ge(S["bq_scaled"], 1)
            for k in range(NQ):
                dve.wait_ge(S["qr_ready"], k + 1)
                nc.vector.scalar_tensor_tensor(v(qrot, k * Q, (SZ, 10), (1, SZ)), bank(4 + k, (SZ, 10), (1, SZ)), HC ** -0.5,
                                               v(bqr, 10 * k, (1, 10), (0, SZ)), ALU.mult, ALU.add
                                               ).then_inc(S["qr_copied"], 1)
            for cc in range(HC):
                dve.wait_ge(gk_in[cc % 3], g_loaded(cc, 3))
                if cc >= 4 and cc % 2 == 0:
                    dve.wait_ge(S["kacc"], cc // 2 - 1)
                if cc >= 3 and cc % 2:
                    dve.wait_ge(S["kpair"], cc // 2)
                for k in range(NQ):
                    dve.wait_ge(S["pq_ready"], NQ * cc + k + 1)
                    nc.vector.scalar_tensor_tensor(v(prod[cc & 3], k * Q, (SZ, 10), (1, SZ)), bank(k, (SZ, 10), (1, SZ)),
                                                   bqs[:, cc:cc + 1], v(gk[cc % 3], 10 * k * PS, (PS, 10), (1, SZ)),
                                                   ALU.add, ALU.mult).then_inc(S["kprod"], 1)
                if cc & 1:
                    a, b = prod[cc & 2], prod[(cc & 2) + 1]
                    dve.wait_ge(S["kprod"], NQ * (cc + 1))
                    tt(a[:], a[:], b[:], ALU.add).then_inc(S["kpair"], 1)

            def boundary_probs(j, o):
                x = px(j, o)
                dve.wait_ge(S["hot"], x + 1)
                nc.vector.tensor_reduce(v(ebd, x, (SZ, SZ)), v(hotp[o & 1], 0, (8, SZ), (1, 8)), AX, ALU.add
                                        ).then_inc(S["eb_red"], 1)

            def evacuate(j, o, at):
                x = px(j, o)
                if at is None or at >= 2:
                    dve.wait_ge(S["shifted"], x - 1)
                for b, (y0, y1, _) in enumerate(YB):
                    dve.wait_ge(S["scores_done"], 3 * x + b + 1)
                    n = y1 - y0
                    tt(v(sc[o & 1], SC * y0, (SC, n), (1, GW)), bank(b, (SW, n), (1, GW), off=SL),
                       cv("neg", (0, n), (1, GW)), ALU.add).then_inc(S["scores_evac"], 1)

            def maxima_waits(j, o):
                x = px(j, o)
                dve.wait_ge(S["scores_evac"], 3 * x + 3)
                dve.wait_ge(S["boundary_in"], x + 1)

            def maxima(j, o, at):
                x = px(j, o)
                nc.vector.copy_predicated(v(sc[o & 1], 0, (SC, SZ), (1, 8)),
                                          cv("hot", (0, SZ), (1, 8)).bitcast(I32),
                                          v(sbx[o & 1], 0, (1, SZ), (0, 8))).then_inc(S["scores_full"], 1)
                dve.wait_ge(S["scores_full"], x + 1)
                if at is None or at >= 2:
                    dve.wait_ge(S["max_t"], x - 1)
                nc.vector.tensor_reduce(v(pmax[o & 1], 0, (8, SZ), (1, 8)), v(sc[o & 1], 0, (SC, SZ), (1, 8), (8, 4)),
                                        AX, ALU.max).then_inc(S["part_max"], 1)

            def column(j, o, at, o_max):
                x = px(j, o)
                if at is None or at + 1 < SZ:
                    maxima_waits(j, o_max)
                dve.wait_ge(S["max_t"], x + 1)
                if at is None or at >= 1:
                    dve.wait_ge(S["max_bc"], x)
                nc.vector.tensor_reduce(cmax[:], bank(4, (C, 3), (1, C)), AX, ALU.max).then_inc(S["col_max"], 1)

            def shift(j, o, at):
                x = px(j, o)
                dve.wait_ge(S["max_bc"], x + 1)
                dve.wait_ge(S["scores_full"], x + 1)
                if at is None or at >= 2:
                    dve.wait_ge(S["exps"], x - 1)
                a, b = gb[o & 1], sc[o & 1]
                tt(v(a, 0, (GW, SZ), (8, 3), (1, 8)), v(b, 0, (SC, SZ), (8, 3), (1, 8)),
                   bank(5, (8, SZ), (0, 3), (1, 8)), ALU.subtract)
                tt(v(a, 24, (GW, SZ), (1, GW - 24)), v(b, 24, (SC, SZ), (1, GW - 24)),
                   bank(5, (8, SZ), (1, GW - 24)), ALU.subtract).then_inc(S["shifted"], 1)

            def weigh(j, o, at):
                x = px(j, o)
                dve.wait_ge(S["exps"], x + 1)
                dve.wait_ge(S["mask_ready"], 4 * x + 4)
                if at is None or at >= 2:
                    dve.wait_ge(S["av_done"], x - 1)
                p_, e_, m_ = pm[o & 1], ex[o & 1], mx[o & 1]
                tt(v(p_, PL, (HC * PW + 1, 2), (PW, HC), (1, GW)), v(e_, 0, (HC * GW, 2), (GW, HC), (1, GW)),
                   v(m_, 0, (HC * GW, 2), (GW, HC), (1, GW)), ALU.mult)
                tt(v(p_, PL + 2 * HC * PW + 2, (PW, 8), (1, GW)), v(e_, 2 * HC * GW, (GW, 8), (1, GW)),
                   v(m_, 2 * HC * GW, (GW, 8), (1, GW)), ALU.mult).then_inc(S["masked"], 1)

            def pick_out(j, o, at):
                x = px(j, o)
                dve.wait_ge(S["av_done"], x + 1)
                if at is None or at >= 1:
                    dve.wait_ge(S["fd_ready"], x)
                tt(osel[:], bank(7, (1, NPS * SZ)), cv("slot_o"), ALU.mult).then_inc(S["o_used"], 1)

            def pick_sum(j, o):
                x = px(j, o)
                dve.wait_ge(S["o_used"], x + 1)
                nc.vector.tensor_reduce(v(frot, x, (SZ, SZ)), v(osel, 0, (NPS, SZ), (1, NPS)), AX, ALU.add
                                        ).then_inc(S["fd_ready"], 1)

            dve.wait_ge(S["zero_buf"], 6)

            def step(j, o, at):
                if on(at, -2):
                    shift(j, o - 2, None if at is None else at - 2)
                if on(at, 0):
                    evacuate(j, o, at)
                if on(at, -5):
                    pick_out(j, o - 5, None if at is None else at - 5)
                if on(at, -4):
                    boundary_probs(j, o - 4)
                if on(at, -5):
                    pick_sum(j, o - 5)
                if on(at, -1):
                    column(j, o - 1, None if at is None else at - 1, o)
                elif on(at, 0):
                    maxima_waits(j, o)
                if on(at, 0):
                    maxima(j, o, at)
                if on(at, -3):
                    weigh(j, o - 3, None if at is None else at - 3)
                if at == SZ + 3:
                    dve.wait_ge(S["eb_red"], SZ)
                    dve.wait_ge(S["eb_mask"], 1)
                    for k in range(NQ):
                        c = slice(k * Q, (k + 1) * Q)
                        tt(ebd[:, c], ebd[:, c], qrot[:, c], ALU.mult).then_inc(S["eb_masked"], 1)
            nc.vector.memset(rt[:], 0.0).then_inc(S["rden"], 1)
            steps(dve, step)


            dve.wait_ge(S["den_done"], SZ)
            dve.wait_ge(S["rden"], 1)
            nc.vector.reciprocal(v(rt, 0, (3, SZ), (1, 2)), bank(6, (3, SZ), (1, 2)))
            nc.vector.reciprocal(v(rt, 2, (3, SZ), parts=64), bank(6, (3, SZ), off=2, parts=64)).then_inc(S["rden"], 1)
            for cc in range(HC):
                dve.wait_ge(gv_in[cc % 5], g_loaded(cc, 5))
                if cc >= 2:
                    dve.wait_ge(S["vacc"], cc - 1)
                for k in range(NQ):
                    dve.wait_ge(S["eb_perm"], k + 1)
                    tt(v(pr[cc & 1], k * Q, (SZ, 10), (1, SZ)), bank(k, (SZ, 10), (1, SZ)),
                       v(gv[cc % 5], 10 * k * PS, (PS, 10), (1, SZ)), ALU.mult).then_inc(S["vprod"], 1)
                if cc == 2:
                    dve.wait_ge(S["rden"], 2)
                    for i, n in enumerate((HC, HC, 8)):
                        tt(v(rexp, i * HC * SZ, (SZ, n), (1, SZ)), v(rt, i, (0, n), (3, SZ)),
                           cv("row_of", (1, n), (0, SZ)), ALU.mult).then_inc(S["rexp_ready"], 1)
            dve.wait_ge(S["nat_in"], 16 * len(ROT))
            dve.wait_ge(S["vacc"], HC)
            for k in range(NQ):
                c = slice(k * Q, (k + 1) * Q)
                tt(sbd[:, c], sbd[:, c], bank(4 + k, (1, Q)), ALU.add).then_inc(S["zsum"], 1)
                dve.wait_ge(S["zsum"], k + 1)
                dve.wait_ge(S["r_nat"], k + 1)
                tt(frot[:, c], sbd[:, c], bank(k, (1, Q)), ALU.mult).then_inc(S["att_nat"], 1)
            for k in range(NQ):
                c = slice(k * Q, (k + 1) * Q)
                dve.wait_ge(S["proj_done"], k + 1)
                nc.vector.scalar_tensor_tensor(xt[:, c], bank(k, (1, Q)), bp[:, 0:1], xt[:, c], ALU.add, ALU.add
                                               ).then_inc(S["resid"], 1)
            dve.wait_ge(S["resid"], NQ)
            norm_vector(dve, NQ, xt, tok, xln)

            count = [0]

            def link(ins, last=False):
                count[0] += 1
                ins.then_inc(S["route"], 1)
                if not last:
                    dve.wait_ge(S["route"], count[0])

            col = lambda i, bc=False: v(lg, 11 * NT * 8 + i * NT, (1, NT), *([(0, 8)] if bc else []), parts=TT)
            iota = cv("iota", (0, NT), (1, 8), parts=TT)
            red = lambda o, i, op: nc.vector.tensor_reduce(o, i, AX, op)
            dve.wait_ge(S["logit_ready"], 1)
            lb = bank(0, (8, NT), (1, 8), parts=TT)
            link(red(col(0), lb, ALU.max))
            link(tt(lgv(1), lb, col(0, True), ALU.subtract))
            dve.wait_ge(S["comb_ready"], 1)
            link(red(col(1), lgv(1), ALU.add))
            link(nc.vector.reciprocal(col(2), col(1)))
            link(tt(lgv(2), lgv(1), col(2, True), ALU.mult))
            for n, (p, eq, oh, top) in enumerate(((lgv(2), lgv(3), lgv(4), 3), (lgv(5), lgv(6), lgv(7), 4))):
                link(red(col(top), p, ALU.max))
                link(tt(eq, p, col(top, True), ALU.is_equal))
                link(nc.vector.scalar_tensor_tensor(eq, eq, -8.0, iota, ALU.mult, ALU.add))
                link(red(col(5 + n), eq, ALU.min))
                link(nc.vector.tensor_scalar(col(5 + n), col(5 + n), 8.0, None, ALU.add))
                link(tt(oh, iota, col(5 + n, True), ALU.is_equal))
                if n == 0:
                    link(nc.vector.scalar_tensor_tensor(lgv(5), oh, -2.0, p, ALU.mult, ALU.add))
            link(tt(col(1), col(3), col(4), ALU.add))
            link(tt(lgv(4), lgv(4), col(3, True), ALU.mult))
            link(tt(lgv(7), lgv(7), col(4, True), ALU.mult))
            link(tt(lgv(4), lgv(4), lgv(7), ALU.add))
            link(nc.vector.tensor_scalar(col(1), col(1), 1e-12, None, ALU.max))
            link(nc.vector.reciprocal(col(2), col(1)))
            link(tt(lgv(0), lgv(4), col(2, True), ALU.mult), last=True)
            assert count[0] == NROUTE, count[0]

            def weighted(k, e, at, weight):
                t = E8 * k + e
                dve.wait_ge(S["gelu_done"], t + 1)
                if at == 0:
                    dve.wait_ge(S["c_ready"], t + 1)
                if e >= 2:
                    dve.wait_ge(S["y_done"], (E8 + 1) * k + e)
                elif at:
                    dve.wait_ge(S["y_done"], (E8 + 1) * k + e - 1)
                tt(hw[e & 1], hb[e], weight, ALU.mult
                   ).then_inc(S["weighted"], 1)

            def finish(k):
                dve.wait_ge(S["y_done"], (E8 + 1) * k + E8 + 1)
                tt(v(tok, k * Q, (1, Q)), v(xt, k * Q, (1, Q)), bank(4, (1, Q)), ALU.add).then_inc(S["y_evac"], 1)

            for e in range(E8):
                weighted(0, e, 0, bank(2 + (e & 1), (1, Q)))
            finish(0)
            for k in range(1, NQ - 1):
                dve.wait_ge(weights_in[k - 1], 16)
            with dve.Fori(0, NQ - 2) as j:
                for e in range(E8):
                    weighted(j + 1, e, 1, weight_slab(j, e))
                finish(j + 1)
            dve.wait_ge(weights_in[NQ - 2], 32)
            for e in range(E8):
                weighted(NQ - 1, e, 1, weight_last(e))
            finish(NQ - 1)


def kernel(x, L0_conv_w_qkv, L0_conv_b_qkv, L0_conv_w_proj, L0_conv_b_proj,
           L0_ffn_router_w, L0_ffn_w1, L0_ffn_b1, L0_ffn_w2, L0_ffn_b2):
    import concourse.bacc as bacc
    from concourse.bass_utils import run_bass_kernel_spmd

    x, wqkv, bqkv = np.asarray(x), np.asarray(L0_conv_w_qkv), np.asarray(L0_conv_b_qkv)
    s = np.arange(C)
    co = 97 * s % C
    rot = (s[:, None] - K * np.arange(SZ)[None]) % C
    q = np.arange(C)
    grp = HC * (q % 8)[:, None] + np.arange(HC)[None]
    t = np.ascontiguousarray
    arrays = {
        "x_in": t(x.reshape(C, L)),
        "wq_t": t(wqkv[0:C].T), "wk_t": t(wqkv[C:2 * C][co].T), "wv_t": t(wqkv[2 * C:3 * C][co].T),
        "wp_t": t(np.asarray(L0_conv_w_proj).T),
        "bq_rot": t(bqkv[0:C][rot]), "bq_s": t(bqkv[0:C][grp]),
        "bkv": t(np.stack([bqkv[C:2 * C][co], bqkv[2 * C:3 * C][co]], 1)),
        "bproj": t(np.asarray(L0_conv_b_proj).reshape(C, 1)),
        "rw_t": t(np.asarray(L0_ffn_router_w).T),
        "w1": t(np.asarray(L0_ffn_w1)), "b1_t": t(np.asarray(L0_ffn_b1).T),
        "w2": t(np.asarray(L0_ffn_w2)), "b2": t(np.asarray(L0_ffn_b2)),
        "ctab": CTAB,
    }
    nc = bacc.Bacc("TRN2", target_bir_lowering=False, num_devices=1)
    args = [nc.dram_tensor(n, list(a.shape), F32, kind="ExternalInput").ap() for n, a in arrays.items()]
    out = nc.dram_tensor("out", [C, L], F32, kind="ExternalOutput").ap()
    program(nc, *args, out)
    got = run_bass_kernel_spmd(nc, [arrays], core_ids=[0]).results[0]["out"]
    return got.reshape(1, C, SZ, SZ)
```

```python
from contextlib import ExitStack

import numpy as np

import concourse.bass as bass
from concourse import mybir

F32 = mybir.dt.float32
I32 = mybir.dt.int32
ALU = mybir.AluOpType
ACT = mybir.ActivationFunctionType
AX = mybir.AxisListType.X

C = 128
HEADS = 8
HC = C // HEADS
SZ = 40
L = SZ * SZ
K = 17
PAD = K // 2
K2 = K * K
PS = SZ + 2 * PAD
IMG = 3168
SLAB = PS * K
NU = (C - 1 + SLAB + C - 1) // C
SKEW = SLAB + C - 1
GW = (C - 1 + K2 - 1) // HC + 1
assert GW == 26 and NU == 9
NEG = -1e30
Q = 400
NQ = L // Q
GROW = (SZ - 1) * PS + SZ
GIMG = GROW + HC - 1
GP = GIMG + 2 * HC
YB = [(0, 14, 0), (14, 27, -1), (27, 40, -2)]
SW, SL = 35, 10
NSL = 10
SC = 32
PW, PL, NPS = 34, 8, 9
PN = PL + PW * SZ + 4
E8 = 8
TT = 100
NT = L // TT


def consts():
    s = np.arange(C)
    co = 97 * s % C
    assert ((K2 * co) % C == s).all()
    base = K2 * co // C
    r, hs = s % HC, s // HC
    w = np.arange(GW)
    y = np.arange(SZ)
    start = HC * w[None] - s[:, None]
    valid = (start >= 0) & (start + HC - 1 <= K2 - 1)
    t = {}
    t["neg"] = np.where(valid, 0.0, NEG)
    l = base[:, None] + np.arange(4)[None]
    dy, dx = l // K - PAD, l % K - PAD
    row = lambda d: (y[None, None] + d[:, :, None] >= 0) & (y[None, None] + d[:, :, None] < SZ)
    rm, cm = row(dy), row(dx)
    t["rv"] = rm[:, w // 8, :].transpose(0, 2, 1) & valid[:, None, :]
    t["cm"] = cm
    t["r0"] = rm[:, 0, :]
    t["hot"] = (hs[:, None] == np.arange(8)[None]) & (r[:, None] != 0)
    p = s[:, None, None]
    yy = y[None, :, None]
    t0 = np.zeros(SZ, int)
    for a, b, f in YB:
        t0[a:b] = f
    j = np.arange(NSL)[None, None] + t0[None, :, None]
    t["slot_q"] = (p >= HC * (j - 1) + yy) & (p < HC * j + yy)
    j = np.arange(NPS)[None, None]
    t["slot_o"] = (p >= HC * (j - 1) + yy % HC) & (p < HC * j + yy % HC)
    t["row_of"] = s[:, None] // 8 == np.arange(HC)[None]
    t["head_of"] = s[:, None] % 8 == s[None] // HC
    t["ident"] = np.eye(C)
    q = np.arange(C)
    t["unperm"] = (HC * (q % 8) + q // 8)[:, None] == s[None]
    t["perm"] = t["unperm"].T
    t["sel"] = (HC * (q % 8) + HC - 1)[:, None] == np.arange(C + HC - 1)[None]
    e = np.zeros((C, E8, C))
    for i in range(E8):
        e[i, i, :] = 1.0
    t["exp"] = e
    t["iota"] = np.broadcast_to(np.arange(8), (C, 8))
    off, at, parts = 0, {}, []
    for n, a in t.items():
        a = np.asarray(a, np.float32).reshape(C, -1)
        at[n] = (off, a.shape[1])
        off += a.shape[1]
        parts.append(a)
    return at, np.ascontiguousarray(np.concatenate(parts, 1))


CAT, CTAB = consts()


def touched(u, a, b):
    ys = [y for y in range(a, b) if 8 * u - GW <= y + y // HC <= 8 * u + 7]
    return (ys[0], ys[-1] + 1) if ys else None


def program(nc, x_in, wq_t, wk_t, wv_t, wp_t, bq_rot, bq_s, bkv, bproj, rw_t, w1, b1_t, w2, b2, ctab, out):
    with ExitStack() as ctx:
        def sb(name, cols, dt=F32):
            return ctx.enter_context(nc.sbuf_tensor(name, [C, cols], dt))

        def sem(name):
            return ctx.enter_context(nc.semaphore(name))

        def dram(name, n):
            return nc.dram_tensor(name, [n], F32, kind="Internal")

        def v(t, off, *dims, parts=C, p0=0):
            pitch = t[:].ap[0][0]
            return bass.AP(t[:].tensor, t[:].offset + p0 * pitch + off, [[pitch, parts]] + [list(d) for d in dims])

        def dv(t, off, *dims):
            return bass.AP(t[:].tensor, off, [list(d) for d in dims])

        con = sb("con", CTAB.shape[1])

        def cv(name, *dims, off=0, parts=C):
            o, n = CAT[name]
            return v(con, o + off, *(dims or [(1, n)]), parts=parts)

        kimg, vimg = sb("kimg", IMG), sb("vimg", IMG)
        xt, xln = sb("xt", L), sb("xln", L)
        qrot, sbd, ebd = sb("qrot", L), sb("sbd", L), sb("ebd", L)
        wide = sb("wide", 2 * L)
        frot, rexp = wide[:, 0:L], wide[:, L:2 * L]
        rt, den = sb("rt", 3 * SZ), sb("den", 3 * SZ)
        dsm = [sb(f"dsm{i}", 3 * C) for i in range(2)]
        tok = frot
        uk = [sb(f"uk{i}", SLAB) for i in range(2)]
        uv = [sb(f"uv{i}", SLAB) for i in range(2)]
        sk = [sb(f"sk{i}", NU * C) for i in range(2)]
        slabs = sb("slabs", 4 * NU * C + 2 * GIMG)
        sv = [slabs[:, i * NU * C:(i + 1) * NU * C] for i in range(2)]
        kt = [slabs[:, (i + 2) * NU * C:(i + 3) * NU * C] for i in range(2)]
        sc = [sb(f"sc{i}", SC * SZ) for i in range(2)]
        ex = [sb(f"ex{i}", GW * SZ) for i in range(2)]
        pm = [sb(f"pm{i}", PN) for i in range(2)]
        hotp = [sb(f"hotp{i}", 8 * SZ) for i in range(2)]
        qs = [sb(f"qs{i}", NSL * SZ) for i in range(2)]
        cmx = [sb(f"cmx{i}", 4) for i in range(2)]
        sbx = [sb(f"sbx{i}", SZ) for i in range(2)]
        pmax = [sb(f"pmax{i}", 3 * C) for i in range(2)]
        cmax = sb("cmax", 3)
        osel = sb("osel", NPS * SZ)
        gb = [slabs[:, 4 * NU * C + i * GIMG:4 * NU * C + (i + 1) * GIMG] for i in range(2)]
        pr = [sb(f"pr{i}", L) for i in range(2)]
        sh = [v(gb[i], 0, (1, GW * SZ)) for i in range(2)]
        mx = pr
        wq2, wk, wv, wp = sb("wq2", 2 * C), sb("wk", C), sb("wv", C), sb("wp", C)
        qspread = [sv, kt]
        prod = [pr[0], pr[1], ebd, pr[1]]
        gk, gv = [gb[0], gb[1], wide], [kimg, vimg, slabs[:, 2 * NU * C:4 * NU * C]]
        bqr, bqs, bk2, bp = sb("bqr", SZ), sb("bqs", HC), sb("bk2", 2), sb("bp", 1)
        rw, b1s, b2s = sb("rw", E8), sb("b1s", E8), sb("b2s", C)
        w1s, w2s = sk
        mean_w = sb("mean_w", C)
        epst = sb("epst", 2)
        stat = sb("stat", 2 * NT)
        hb = [v((kimg, vimg)[e // 4], e % 4 * Q, (1, Q)) for e in range(E8)]
        hw = [v(sc[1], i * Q, (1, Q)) for i in range(2)]
        lg = rexp
        combt = sbd

        ps = ctx.enter_context(nc.psum_tensor("ps", [C, 8 * 512], F32))

        def bank(b, *dims, off=0, parts=C):
            return v(ps, 512 * b + off, *dims, parts=parts)

        krd, kld, vrd, vld = (dram(n, (C + 9) * GP) for n in ("krd", "kld", "vrd", "vld"))
        ksl, vsl = dram("ksl", SZ * C * SLAB), dram("vsl", SZ * C * SLAB)
        frd = dram("frd", 2 * C * L)
        combd = dram("combd", E8 * L)

        names = """x_in w_kv w_q w_late consts const_set zero_img zero_buf
            mean_ready centred sq_ready var_ready std_ready rstd_ready rstd_spread normed
            k_ready v_ready k_copied v_copied qr_ready qr_copied bq_scaled
            qt_ready qt_copied q_spread
            shift_k shift_v
            pq_ready kprod kpair kacc sb_copied
            slab_copied kt_ready kt_copied scores_done scores_evac scores_full part_max max_t col_max
            max_bc shifted exps boundary_in colmask_in head_sum mask_ready q_slots hot masked
            den_done den_summed dsm_zero av_done o_used
            fd_ready eb_red eb_mask eb_masked eb_perm vprod vacc rot_out nat_in zsum rden
            rexp_ready r_nat att_nat proj_done
            resid logit_ready route comb_ready comb_t comb_copied
            h_ready comb_out c_ready gelu_done weighted y_done y_evac y_sum out_sent""".split()
        S = {n: sem(n) for n in names}
        stored = [sem(f"stored{i}") for i in range(2)]
        skewk = [sem(f"skewk{i}") for i in range(2)]
        skewv = [sem(f"skewv{i}") for i in range(2)]
        lastv = [sem(f"lastv{i}") for i in range(2)]
        weights_in = [sem(f"weights_in{k}") for k in range(1, NQ)]
        gk_in = [sem(f"gk_in{i}") for i in range(3)]
        gv_in = [sem(f"gv_in{i}") for i in range(3)]
        block = ctx.enter_context(nc.Block())

        def px(j, o):
            return 2 * j + o

        def half(j, o):
            return j + (o >> 1)

        FULL_LO, FULL_HI = 6, 36

        def steps(eng, fn):
            for o in range(FULL_LO):
                fn(0, o, o)
            with eng.Fori(FULL_LO // 2, FULL_HI // 2) as j:
                for o in range(2):
                    fn(j, o, None)
            for o in range(FULL_HI, SZ + 5):
                fn(0, o, o)

        def on(at, d):
            return at is None or 0 <= at + d < SZ

        def shifted_images(eng, img, right, left, done):
            eng.dma_start(dv(right, HC, (GP, 8), (8 * GP + 1, HC), (1, GIMG)), v(img, 0, (1, GIMG))).then_inc(done, 16)
            at, n = 2 * PAD * PS + K - (HC - 1), GIMG + HC - 1
            for h, p0, heads in ((2, 0, 6), (0, 6 * HC, 2)):
                eng.dma_start(dv(left, (8 + h) * GP + HC + 1 - (HC - 1), (GP, heads), (8 * GP + 1, HC), (1, n)),
                              v(img, at, (1, n), parts=HC * heads, p0=p0)).then_inc(done, 16)

        NSHIFT = 3
        ROT = []
        for y in range(SZ):
            if not ROT or K * y // C != K * ROT[-1][0] // C:
                ROT.append([y, y])
            ROT[-1][1] = y + 1

        NG = len(gk)

        def load_g(eng, right, left, cc, bufs, done):
            g, n = bufs[cc % NG], 8 * (cc + 1)
            first = 0 if cc < NG else n - 8 * NG
            eng.dma_start(v(g, cc, (1, GIMG - cc), parts=n - first, p0=first),
                          dv(right, first * GP + HC + cc, (GP, n - first), (1, GIMG - cc))).then_inc(done[cc % NG], 16)
            if cc < NG:
                eng.dma_start(v(g, cc, (1, GIMG - cc), parts=C - n, p0=n),
                              dv(left, n * GP + HC + cc, (GP, C - n), (1, GIMG - cc))).then_inc(done[cc], 16)

        def g_loaded(cc):
            return 16 * (2 + cc // NG)

        def weight_slab(j, e):
            return v(slabs, 2 * Q * e + Q * j, (1, Q))

        def weight_last(e):
            return v((qrot, ebd)[e // 4], e % 4 * Q, (1, Q))

        def lgv(i, *dims):
            return v(lg, i * NT * 8, *(dims or [(8, NT), (1, 8)]), parts=TT)

        mm = nc.tensor.matmul

        ROTATED_WITH = {0: (1,), 1: (2,), 2: (3,)}

        def kt_bank(g, at):
            return (3, 2 if at == 0 else 4, 3)[g]

        NROUTE = 26

        @block.sync
        def _(sp):
            sp.wait_ge(S["const_set"], 4)
            for k in range(NQ):
                sp.dma_start(xt[:, k * Q:(k + 1) * Q], x_in[:, k * Q:(k + 1) * Q]).then_inc(S["x_in"], 16)
            sp.dma_start(wk[:], wk_t).then_inc(S["w_kv"], 16)
            sp.dma_start(wv[:], wv_t).then_inc(S["w_kv"], 16)
            sp.dma_start(bk2[:], bkv).then_inc(S["w_kv"], 16)
            sp.dma_start(bp[:], bproj).then_inc(S["w_late"], 16)
            sp.dma_start(wp[:], wp_t).then_inc(S["w_late"], 16)
            sp.dma_start(rw[:], rw_t).then_inc(S["w_late"], 16)
            sp.dma_start(b1s[:], b1_t).then_inc(S["w_late"], 16)
            sp.dma_start(b2s[0:E8, :], b2).then_inc(S["w_late"], 16)

            sp.wait_ge(S["k_copied"], NQ)
            shifted_images(sp, kimg, krd, kld, S["shift_k"])
            def store(j, o):
                x = px(j, o)
                sp.wait_ge(S["slab_copied"], 2 * x + 2)
                sp.dma_start(dv(ksl, x * (C * SLAB), (SLAB, C), (1, SLAB)), uk[o & 1][:]).then_inc(stored[o & 1], 16)
                sp.dma_start(dv(vsl, x * (C * SLAB), (SLAB, C), (1, SLAB)), uv[o & 1][:]).then_inc(stored[o & 1], 16)

            def load_k(j, o, at):
                x = px(j, o)
                sp.wait_ge(stored[o & 1], 32 * half(j, o) + 32)
                if at is None or at >= 2:
                    sp.wait_ge(S["kt_ready"], 3 * x - 3)
                sp.dma_start(v(sk[o & 1], 0, (1, SKEW)),
                             dv(ksl, x * (C * SLAB), (SLAB - 1, C), (1, SKEW))).then_inc(skewk[o & 1], 16)

            def load_v(j, o, at):
                x = px(j, o)
                if at is None or at >= 2:
                    sp.wait_ge(S["av_done"], x - 1)
                sp.wait_ge(stored[o & 1], 32 * half(j, o) + 32)
                sp.dma_start(v(sv[o & 1], 0, (1, SKEW)),
                             dv(vsl, x * (C * SLAB), (SLAB - 1, C), (1, SKEW))).then_inc(skewv[o & 1], 16)

            sp.wait_ge(S["shift_k"], NSHIFT * 16)
            for cc in range(HC):
                if cc >= 3:
                    sp.wait_ge(S["kprod"], NQ * (cc - 2))
                load_g(sp, krd, kld, cc, gk, gk_in)
                if cc == NG - 1:
                    store(0, 0)
                    store(0, 1)
                if cc == 3:
                    sp.wait_ge(S["zero_buf"], 6)
                    load_k(0, 0, 0)
                    load_k(0, 1, 1)
                if cc == 9:
                    store(0, 2)
                    store(0, 3)
            load_k(0, 2, 2)

            def step(j, o, at):
                if on(at, 3):
                    load_k(j, o + 3, None if at is None else at + 3)
                if on(at, 4):
                    store(j, o + 4)
                if at == SZ - 2:
                    for x in (SZ - 2, SZ - 1):
                        sp.wait_ge(S["kt_ready"], 3 * x + 3)
                        sp.wait_ge(stored[x & 1], 32 * (x // 2) + 32)
                        sp.dma_start(v(sk[x & 1], 0, (1, SKEW)),
                                     dv(vsl, x * (C * SLAB), (SLAB - 1, C), (1, SKEW))).then_inc(lastv[x & 1], 16)
                if on(at, -2) and (at is None or at < SZ):
                    load_v(j, o - 2, None if at is None else at - 2)
                if at in (38, 39):
                    sp.wait_ge(S["slab_copied"], 2 * SZ)
                    sp.wait_ge(S["shift_v"], NSHIFT * 16)
                    load_g(sp, vrd, vld, at - 38, gv, gv_in)
                if at == 40:
                    sp.wait_ge(S["scores_done"], 3 * SZ)
                    load_g(sp, vrd, vld, 2, gv, gv_in)
                if at == FULL_HI:
                    sp.wait_ge(S["v_copied"], NQ)
                    shifted_images(sp, vimg, vrd, vld, S["shift_v"])

            steps(sp, step)

            sp.wait_ge(S["fd_ready"], SZ)
            for i in range(2):
                sp.dma_start(dv(frd, i * C * L, (L, C), (1, L)), frot[:]).then_inc(S["rot_out"], 16)
            for cc in range(NG, HC):
                sp.wait_ge(S["vprod"], NQ * (cc - NG + 1))
                load_g(sp, vrd, vld, cc, gv, gv_in)
                if cc == 6:
                    sp.wait_ge(S["rot_out"], 32)
                    sp.wait_ge(S["boundary_in"], SZ)
                    for y0, y1 in ROT:
                        r0 = K * y0 % C
                        sp.dma_start(v(sbd, y0 * SZ, (SZ, y1 - y0), (1, SZ)),
                                     dv(frd, r0 * L + y0 * SZ, (L, C), (K * L + SZ, y1 - y0), (1, SZ))
                                     ).then_inc(S["nat_in"], 16)
                if cc == 8:
                    sp.wait_ge(S["av_done"], SZ)
                    sp.dma_start(v(w1s, 0, (C, E8), (1, C)), w1.rearrange("e d f -> d e f")).then_inc(S["w_late"], 16)
                    sp.dma_start(v(w2s, 0, (C, E8), (1, C)), w2.rearrange("e d f -> d e f")).then_inc(S["w_late"], 16)

            sp.wait_ge(S["comb_copied"], NQ)
            sp.dma_start(dv(combd, 0, (L, E8), (1, L)), v(combt, 0, (1, L), parts=E8)).then_inc(S["comb_out"], 16)
            sp.wait_ge(S["comb_out"], 16)
            for k in range(1, NQ - 1):
                sp.dma_start(v(slabs, (k - 1) * Q, (2 * Q, E8), (1, Q)),
                             dv(combd, k * Q, (0, C), (L, E8), (1, Q))).then_inc(weights_in[k - 1], 16)
            for i in range(2):
                sp.dma_start(v((qrot, ebd)[i], 0, (Q, 4), (1, Q)),
                             dv(combd, 4 * i * L + (NQ - 1) * Q, (0, C), (L, 4), (1, Q))).then_inc(weights_in[NQ - 2], 16)

            for k in range(NQ):
                sp.wait_ge(S["y_sum"], k + 1)
                sp.dma_start(out[:, k * Q:(k + 1) * Q], xln[:, k * Q:(k + 1) * Q]).then_inc(S["out_sent"], 16)
            sp.wait_ge(S["out_sent"], 16 * NQ)

        @block.gpsimd
        def _(pool):
            nc.gpsimd.memset(kimg[:], 0.0).then_inc(S["zero_img"], 1)
            nc.gpsimd.memset(vimg[:], 0.0).then_inc(S["zero_img"], 1)
            pool.wait_ge(S["x_in"], 16 * NQ)
            pool.dma_start(con[:], ctab).then_inc(S["consts"], 16)
            for i in range(2):
                nc.gpsimd.memset(v(sk[i], SKEW, (1, NU * C - SKEW)), 0.0).then_inc(S["zero_buf"], 1)
                nc.gpsimd.memset(v(sv[i], SKEW, (1, NU * C - SKEW)), 0.0).then_inc(S["zero_buf"], 1)
                nc.gpsimd.memset(pm[i][:], 0.0).then_inc(S["zero_buf"], 1)

            def slots(j, o, at):
                x = px(j, o)
                if at is None or at >= 2:
                    pool.wait_ge(S["scores_done"], 3 * x - 3)
                nc.gpsimd.tensor_tensor(v(qs[o & 1], 0, (NSL, SZ), (1, NSL)), cv("slot_q", (NSL, SZ), (1, NSL)),
                                        v(qrot, x, (SZ, SZ), (0, NSL)), ALU.mult).then_inc(S["q_slots"], 1)

            def fetch_scores(j, o, at):
                x = px(j, o)
                if at is None or at >= 2:
                    pool.wait_ge(S["scores_full"], x - 1)
                nc.gpsimd.tensor_copy(sbx[o & 1][:], v(sbd, x, (SZ, SZ))).then_inc(S["boundary_in"], 1)

            def fetch_mask(j, o, at):
                x = px(j, o)
                if at is None or at >= 2:
                    pool.wait_ge(S["mask_ready"], 4 * x - 4)
                nc.gpsimd.tensor_copy(cmx[o & 1][:], v(con, CAT["cm"][0] + x, (SZ, 4))).then_inc(S["colmask_in"], 1)

            def pick(j, o, at):
                x = px(j, o)
                pool.wait_ge(S["exps"], x + 1)
                if at is None or at >= 2:
                    pool.wait_ge(S["eb_red"], x - 1)
                nc.gpsimd.tensor_tensor(v(hotp[o & 1], 0, (8, SZ), (1, 8)), v(ex[o & 1], 0, (GW, SZ), (1, 8)),
                                        cv("hot", (0, SZ), (1, 8)), ALU.mult).then_inc(S["hot"], 1)

            def sum_heads(j, o, at):
                x = px(j, o)
                d, e = dsm[o & 1], ex[o & 1]
                if at is None or at >= 2:
                    pool.wait_ge(S["den_done"], x - 1)
                nc.gpsimd.tensor_tensor(v(d, 0, (8, SZ), (1, 8)), v(e, 0, (GW, SZ), (1, 8)), v(e, 8, (GW, SZ), (1, 8)),
                                        ALU.add).then_inc(S["head_sum"], 1)
                for m, n in ((2, 8), (3, 2)):
                    pool.wait_ge(S["head_sum"], 3 * x + m - 1)
                    nc.gpsimd.tensor_tensor(v(d, 0, (8, SZ), (1, n)), v(d, 0, (8, SZ), (1, n)),
                                            v(e, 8 * m, (GW, SZ), (1, n)), ALU.add).then_inc(S["head_sum"], 1)

            pool.wait_ge(S["dsm_zero"], 2)
            pool.wait_ge(S["consts"], 16)
            pool.wait_ge(S["qr_copied"], NQ)
            slots(0, 0, 0)
            slots(0, 1, 1)
            pool.wait_ge(S["sb_copied"], NQ)
            fetch_scores(0, 0, 0)

            def step(j, o, at):
                if on(at, 1):
                    fetch_scores(j, o + 1, None if at is None else at + 1)
                if on(at, -1):
                    fetch_mask(j, o - 1, None if at is None else at - 1)
                if on(at, 2):
                    slots(j, o + 2, None if at is None else at + 2)
                if at == SZ - 1:
                    pool.wait_ge(S["q_slots"], SZ)
                    nc.gpsimd.tensor_tensor(v(qrot, 0, (SZ, SZ), (1, SZ)), cv("r0", (1, SZ), (0, SZ)),
                                            cv("cm", (0, SZ), (1, SZ)), ALU.mult).then_inc(S["eb_mask"], 1)
                if on(at, -3):
                    pick(j, o - 3, None if at is None else at - 3)
                    sum_heads(j, o - 3, None if at is None else at - 3)

            steps(pool, step)
            for k in range(NQ):
                pool.wait_ge(S["y_evac"], k + 1)
                nc.gpsimd.tensor_tensor(xln[:, k * Q:(k + 1) * Q], xln[:, k * Q:(k + 1) * Q],
                                        tok[:, k * Q:(k + 1) * Q], ALU.add).then_inc(S["y_sum"], 1)

        def norm_scalar(act, n0, src, dst, eps):
            for k in range(NQ):
                act.wait_ge(S["centred"], n0 + k + 1)
                nc.scalar.activation(dst[:, k * Q:(k + 1) * Q], src[:, k * Q:(k + 1) * Q], ACT.Square
                                     ).then_inc(S["sq_ready"], 1)
            act.wait_ge(S["var_ready"], n0 // NQ + 1)
            nc.scalar.activation(v(stat, 0, (1, NT), parts=TT), bank(0, (1, NT), parts=TT), ACT.Sqrt,
                                 bias=epst[0:TT, eps:eps + 1]).then_inc(S["std_ready"], 1)

        @block.scalar
        def _(act):
            act.dma_start(wq2[:, 0:C], wq_t).then_inc(S["w_q"], 16)
            act.dma_start(wq2[:, C:2 * C], wq_t).then_inc(S["w_q"], 16)
            act.dma_start(bqr[:], bq_rot).then_inc(S["w_q"], 16)
            act.dma_start(bqs[:], bq_s).then_inc(S["w_q"], 16)
            act.wait_ge(S["const_set"], 3)
            nc.scalar.activation(stat[0:1, 0:1], epst[0:1, 1:2], ACT.Sqrt)
            norm_scalar(act, 0, tok, pr[0], 0)
            act.wait_ge(S["w_kv"], 48)
            for dst, b, ready, copied, zero in ((kimg, 0, "k_ready", "k_copied", 1), (vimg, 1, "v_ready", "v_copied", 2)):
                if b:
                    for k in range(NQ):
                        act.wait_ge(S["qt_ready"], k + 1)
                        nc.scalar.activation(v(ex[k // 2], (k % 2) * 4 * C, (1, 4 * C), parts=TT),
                                             bank(4 + k, (1, 4 * C), parts=TT), ACT.Copy).then_inc(S["qt_copied"], 1)
                act.wait_ge(S["zero_img"], zero)
                for k in range(NQ):
                    act.wait_ge(S[ready], k + 1)
                    nc.scalar.activation(v(dst, (PAD + 10 * k) * PS + PAD, (PS, 10), (1, SZ)),
                                         bank(k, (SZ, 10), (1, SZ)), ACT.Identity,
                                         bias=bk2[:, b:b + 1]).then_inc(S[copied], 1)

            def slab(j, o, at):
                x = px(j, o)
                if at is None or at >= 2:
                    act.wait_ge(stored[o & 1], 32 * half(j, o))
                nc.scalar.activation(v(uk[o & 1], 0, (K, PS), (1, K)), v(kimg, x, (PS, PS), (1, K)), ACT.Copy
                                     ).then_inc(S["slab_copied"], 1)
                nc.scalar.activation(v(uv[o & 1], 0, (K, PS), (1, K)), v(vimg, x, (PS, PS), (1, K)), ACT.Copy
                                     ).then_inc(S["slab_copied"], 1)

            def kt_copy(j, o, at, g):
                x = px(j, o)
                if g == 0 and (at is None or at >= 2):
                    act.wait_ge(S["scores_done"], 3 * x - 3)
                act.wait_ge(S["kt_ready"], 3 * x + g + 1)
                n = (4, 4, 1)[g] * C
                nc.scalar.activation(v(kt[o & 1], 4 * g * C, (1, n)), bank(kt_bank(g, at), (1, n)), ACT.Copy
                                     ).then_inc(S["kt_copied"], 1)

            def exps(j, o, at):
                x = px(j, o)
                act.wait_ge(S["shifted"], x + 1)
                if at is None or at >= 2:
                    act.wait_ge(S["masked"], x - 1)
                    act.wait_ge(S["head_sum"], 3 * x - 3)
                    act.wait_ge(S["hot"], x - 1)
                nc.scalar.activation(ex[o & 1][:], sh[o & 1], ACT.Exp
                                     ).then_inc(S["exps"], 1)

            def mask(j, o, at):
                x = px(j, o)
                act.wait_ge(S["colmask_in"], x + 1)
                act.wait_ge(S["consts"], 16)
                if at is None or at >= 2:
                    act.wait_ge(S["masked"], x - 1)
                for m in range(4):
                    n = min(8, GW - 8 * m)
                    nc.scalar.activation(v(mx[o & 1], 8 * m, (GW, SZ), (1, n)), cv("rv", (GW, SZ), (1, n), off=8 * m),
                                         ACT.Copy, scale=cmx[o & 1][:, m:m + 1]).then_inc(S["mask_ready"], 1)

            act.wait_ge(S["k_copied"], NQ)
            act.wait_ge(S["v_copied"], NQ)
            act.wait_ge(S["qt_copied"], NQ)
            for cc in range(HC):
                if cc >= 2:
                    act.wait_ge(S["pq_ready"], NQ * (cc - 1))
                if cc == 2:
                    slab(0, 0, 0)
                    slab(0, 1, 1)
                if cc == 8:
                    slab(0, 2, 2)
                    slab(0, 3, 3)
                for i in range(2):
                    nc.scalar.activation(v(qspread[cc & 1][i], 0, (C, 8), (8, HC), (1, 8), parts=TT),
                                         v(ex[i], cc, (C, 8), (0, HC), (HC, 8), parts=TT), ACT.Copy
                                         ).then_inc(S["q_spread"], 1)
            for g in range(3):
                kt_copy(0, 0, 0, g)
            for k in range(NQ):
                act.wait_ge(S["kacc"], HC // 2)
                nc.scalar.mul(sbd[:, k * Q:(k + 1) * Q], bank(4 + k, (1, Q)), HC ** -0.5).then_inc(S["sb_copied"], 1)
            for g in range(3):
                kt_copy(0, 1, 1, g)

            def step(j, o, at):
                if on(at, 4):
                    slab(j, o + 4, None if at is None else at + 4)
                if on(at, 2):
                    kt_copy(j, o + 2, None if at is None else at + 2, 0)
                    kt_copy(j, o + 2, None if at is None else at + 2, 1)
                if on(at, -2):
                    exps(j, o - 2, None if at is None else at - 2)
                if on(at, 2):
                    kt_copy(j, o + 2, None if at is None else at + 2, 2)
                if on(at, -2):
                    mask(j, o - 2, None if at is None else at - 2)

            steps(act, step)

            nc.scalar.activation(stat[0:1, 0:1], epst[0:1, 1:2], ACT.Sqrt)
            norm_scalar(act, NQ, tok, pr[0], 1)
            act.wait_ge(S["route"], 3)
            nc.scalar.activation(lgv(1), lgv(1), ACT.Exp).then_inc(S["comb_ready"], 1)
            def gelu(k, e, at):
                t = E8 * k + e
                act.wait_ge(S["h_ready"], t + 1)
                if at:
                    act.wait_ge(S["weighted"], t - (E8 - 1))
                nc.scalar.activation(hb[e], bank(e & 3 if at else e % 3, (1, Q)), ACT.Gelu, bias=b1s[:, e:e + 1]
                                     ).then_inc(S["gelu_done"], 1)

            for e in range(E8):
                gelu(0, e, 0)
            for k in range(NQ):
                act.wait_ge(S["comb_t"], k + 1)
                nc.scalar.activation(v(combt, k * Q, (1, Q), parts=E8), bank(4 + k, (1, Q), parts=E8), ACT.Copy
                                     ).then_inc(S["comb_copied"], 1)
            with act.Fori(1, NQ) as k:
                for e in range(E8):
                    gelu(k, e, 1)

        def norm_tensor(pe, n0, src, waits, between=lambda: None):
            for k in range(NQ):
                for s_, n in waits(k):
                    pe.wait_ge(s_, n)
                mm(bank(k, (1, Q)), mean_w[:], src[:, k * Q:(k + 1) * Q], start=True, stop=True
                   ).then_inc(S["mean_ready"], 1)
            pe.wait_ge(S["centred"], n0 + NQ)
            for t in range(NT):
                pe.wait_ge(S["sq_ready"], n0 + t * TT // Q + 1)
                last = mm(bank(0, (1, 1), off=t, parts=TT), pr[0][:, t * TT:(t + 1) * TT], mean_w[:, 0:1],
                          start=True, stop=True, skip_group_check=True)
            last.then_inc(S["var_ready"], 1)
            between()
            if n0 == 0:
                pe.wait_ge(S["consts"], 16)
            pe.wait_ge(S["rstd_ready"], n0 // NQ + 1)
            for t in range(NT):
                last = nc.tensor.transpose(bank(4 + t * TT // Q, (1, TT), off=t * TT % Q), v(stat, NT + t, (0, C), parts=TT),
                                           cv("ident", (1, TT), parts=TT))
                if (t + 1) * TT % Q == 0:
                    last.then_inc(S["rstd_spread"], 1)

        @block.tensor
        def _(pe):
            pe.wait_ge(S["const_set"], 3)
            norm_tensor(pe, 0, xt, lambda k: [(S["x_in"], 16 * NQ)])
            pe.wait_ge(S["w_kv"], 48)
            for k in range(NQ):
                pe.wait_ge(S["normed"], k + 1)
                mm(bank(k, (1, Q)), wk[:], xln[:, k * Q:(k + 1) * Q], start=True, stop=True).then_inc(S["k_ready"], 1)
            pe.wait_ge(S["w_q"], 64)
            for t in range(NT):
                last = mm(bank(4 + t // 4, (1, C), off=C * (t % 4), parts=TT), xln[:, t * TT:(t + 1) * TT], wq2[:, 0:C],
                          start=True, stop=True, skip_group_check=True)
                if t % 4 == 3:
                    last.then_inc(S["qt_ready"], 1)
            for k in range(NQ):
                pe.wait_ge(S["k_copied"], k + 1)
                mm(bank(k, (1, Q)), wv[:], xln[:, k * Q:(k + 1) * Q], start=True, stop=True).then_inc(S["v_ready"], 1)

            def rotated_q(k):
                pe.wait_ge(S["qt_copied"], k + 1)
                for y in range(10 * k, 10 * k + 10):
                    rho = K * y % C
                    last = mm(bank(4 + k, (1, SZ), off=SZ * (y % 10)), wq2[:, C - rho:2 * C - rho],
                              xln[:, y * SZ:(y + 1) * SZ], start=True, stop=True, skip_group_check=True)
                last.then_inc(S["qr_ready"], 1)

            def transposes(j, o, at, g):
                x = px(j, o)
                if g == 0:
                    pe.wait_ge(skewk[o & 1], 16 * half(j, o) + 16)
                    if at is None or at >= 1:
                        pe.wait_ge(S["kt_copied"], 3 * x)
                if g == 1:
                    if at is None or at >= 1:
                        pe.wait_ge(S["kt_copied"], 3 * x - 1)
                    if at is None or at >= 4:
                        pe.wait_ge(S["col_max"], x - 3)
                if g == 2:
                    pe.wait_ge(S["kt_copied"], 3 * x + 1)
                for i in range((4, 4, 1)[g]):
                    last = nc.tensor.transpose(bank(kt_bank(g, at), (1, C), off=i * C),
                                               v(sk[o & 1], (4 * g + i) * C, (1, C)), cv("ident"))
                last.then_inc(S["kt_ready"], 1)

            rotated_q(0)
            for cc in range(HC + 2):
                for k in range(NQ):
                    if cc < HC:
                        if cc == 0:
                            pe.wait_ge(S["v_copied"], k + 1)
                        else:
                            pe.wait_ge(S["kprod"], NQ * (cc - 1) + k + 1)
                        pe.wait_ge(S["q_spread"], 2 * cc + k // 2 + 1)
                        for i in range(4):
                            t = 4 * k + i
                            last = nc.tensor.transpose(bank(k, (1, TT), off=TT * i),
                                                       v(qspread[cc & 1][t // 8], (t % 8) * C, (1, C), parts=TT),
                                                       cv("ident", (1, TT), parts=TT))
                        last.then_inc(S["pq_ready"], 1)
                for k in ROTATED_WITH.get(cc, ()):
                    rotated_q(k)
                if cc >= 2:
                    pair = cc // 2 - 1
                    pe.wait_ge(S["kpair"], pair + 1)
                    for k in (0, 1) if cc % 2 == 0 else (2, 3):
                        if pair == 0:
                            pe.wait_ge(S["qr_copied"], k + 1)
                        last = mm(bank(4 + k, (1, Q)), cv("unperm"), prod[2 * pair & 3][:, k * Q:(k + 1) * Q],
                                  start=(pair == 0), stop=(2 * pair == HC - 2), skip_group_check=True)
                    if cc & 1:
                        last.then_inc(S["kacc"], 1)
                if cc == HC - 1:
                    pe.wait_ge(S["kprod"], NQ * HC)
                    transposes(0, 0, 0, 0)
                    transposes(0, 0, 0, 1)

            def scores(j, o, at, banks):
                x = px(j, o)
                if banks[0] == 0:
                    pe.wait_ge(S["kt_copied"], 3 * x + 3)
                    pe.wait_ge(S["q_slots"], x + 1)
                for b in banks:
                    y0, y1, t0 = YB[b]
                    if at is None or at >= 1:
                        pe.wait_ge(S["scores_evac"], 3 * x - 2 + b)
                    parts = [(u, *touched(u, y0, y1)) for u in range(NU) if touched(u, y0, y1)]
                    for n, (u, a, z) in enumerate(parts):
                        at0 = SL + SW * (a - y0) + 8 * u + t0 - 1 - a
                        last = mm(bank(b, (SW - 1, z - a), (1, NSL), off=at0), v(kt[o & 1], u * C, (1, C)),
                                  v(qs[o & 1], a * NSL, (NSL, z - a), (1, NSL)),
                                  start=(n == 0), stop=(n == len(parts) - 1), skip_group_check=True)
                    last.then_inc(S["scores_done"], 1)

            def max_t(j, o, at):
                x = px(j, o)
                pe.wait_ge(S["part_max"], x + 1)
                pe.wait_ge(S["kt_copied"], 3 * x + 11 if (at is None or at + 3 < SZ) else 3 * SZ - 1)
                for i in range(3):
                    last = nc.tensor.transpose(bank(4, (1, C), off=i * C), pmax[o & 1][:, i * C:(i + 1) * C], cv("ident"))
                last.then_inc(S["max_t"], 1)

            def max_bc(j, o, at):
                x = px(j, o)
                pe.wait_ge(S["col_max"], x + 1)
                if at is None or at >= 1:
                    pe.wait_ge(S["shifted"], x)
                for i, n in enumerate((C, C, 64)):
                    last = nc.tensor.transpose(bank(5, (1, n), off=i * C), v(cmax, i, (0, C), parts=n),
                                               cv("ident", (1, n), parts=n))
                last.then_inc(S["max_bc"], 1)

            def sums(j, o, at):
                x = px(j, o)
                pe.wait_ge(S["head_sum"], 3 * x + 3)
                if at is None or at >= 1:
                    pe.wait_ge(S["den_summed"], x)
                for i in range(3):
                    last = nc.tensor.transpose(bank(6, (1, C), off=i * C), v(dsm[o & 1], i * C, (1, C)), cv("ident"))
                last.then_inc(S["den_done"], 1)

            def products(j, o, at):
                x = px(j, o)
                pe.wait_ge(S["masked"], x + 1)
                late = at is not None and at >= SZ - 2
                pe.wait_ge(*((lastv[o & 1], 16) if late else (skewv[o & 1], 16 * half(j, o) + 16)))
                if at is None or at >= 1:
                    pe.wait_ge(S["o_used"], x)
                for u in range(NU):
                    a, z = touched(u, 0, SZ)
                    at0 = PL + PW * a + 8 * u - 1 - a
                    last = mm(bank(7, (1, NPS * (z - a)), off=NPS * a), v((sk if late else sv)[o & 1], u * C, (1, C)),
                              v(pm[o & 1], at0, (PW - 1, z - a), (1, NPS)),
                              start=(u == 0), stop=(u == NU - 1), skip_group_check=True)
                last.then_inc(S["av_done"], 1)

            transposes(0, 0, 0, 2)
            scores(0, 0, 0, range(3))
            pe.wait_ge(S["sb_copied"], NQ)
            for g in range(3):
                transposes(0, 1, 1, g)

            def step(j, o, at):
                if on(at, 2):
                    transposes(j, o + 2, None if at is None else at + 2, 0)
                    transposes(j, o + 2, None if at is None else at + 2, 1)
                if on(at, -4):
                    sums(j, o - 4, None if at is None else at - 4)
                if on(at, 1):
                    scores(j, o + 1, None if at is None else at + 1, (0,))
                if on(at, 2):
                    transposes(j, o + 2, None if at is None else at + 2, 2)
                if on(at, -1):
                    max_t(j, o - 1, None if at is None else at - 1)
                if on(at, 1):
                    scores(j, o + 1, None if at is None else at + 1, (1, 2))
                if on(at, -1):
                    max_bc(j, o - 1, None if at is None else at - 1)
                if on(at, -4):
                    products(j, o - 4, None if at is None else at - 4)

            steps(pe, step)

            pe.wait_ge(S["shifted"], SZ)
            pe.wait_ge(S["scores_evac"], 3 * SZ)
            pe.wait_ge(S["kt_copied"], 3 * SZ)
            for k in range(NQ):
                pe.wait_ge(S["eb_masked"], k + 1)
                mm(bank(k, (1, Q)), cv("perm"), ebd[:, k * Q:(k + 1) * Q], start=True, stop=True
                   ).then_inc(S["eb_perm"], 1)
            pe.wait_ge(S["fd_ready"], SZ)
            pe.wait_ge(S["rden"], 2)
            for cc in range(HC):
                for k in range(NQ):
                    pe.wait_ge(S["vprod"], NQ * cc + k + 1)
                    last = mm(bank(4 + k, (1, Q)), cv("sel", (1, C), off=HC - 1 - cc),
                              pr[cc & 1][:, k * Q:(k + 1) * Q], start=(cc == 0), stop=(cc == HC - 1),
                              skip_group_check=True)
                last.then_inc(S["vacc"], 1)

            pe.wait_ge(S["vprod"], NQ * HC)
            for k in range(NQ):
                pe.wait_ge(S["rexp_ready"], 3)
                mm(bank(k, (1, Q)), cv("head_of"), rexp[:, k * Q:(k + 1) * Q], start=True, stop=True
                   ).then_inc(S["r_nat"], 1)
            pe.wait_ge(S["w_late"], 16 * 7)
            for k in range(NQ):
                pe.wait_ge(S["att_nat"], k + 1)
                mm(bank(k, (1, Q)), wp[:], frot[:, k * Q:(k + 1) * Q], start=True, stop=True
                   ).then_inc(S["proj_done"], 1)

            def logits():
                for t in range(NT):
                    last = mm(bank(3, (1, 8), off=8 * t, parts=TT), tok[:, t * TT:(t + 1) * TT], rw[:],
                              start=True, stop=True, skip_group_check=True)
                last.then_inc(S["logit_ready"], 1)

            norm_tensor(pe, NQ, xt, lambda k: [(S["resid"], k + 1)], logits)
            pe.wait_ge(S["normed"], NQ + 1)

            def up(k, e, at):
                t = E8 * k + e
                if at:
                    pe.wait_ge(S["gelu_done"], t - 3)
                elif e >= 3:
                    pe.wait_ge(S["gelu_done"], e - 2)
                mm(bank(e & 3 if at else e % 3, (1, Q)), v(w1s, e * C, (1, C)), v(xln, k * Q, (1, Q)),
                   start=True, stop=True).then_inc(S["h_ready"], 1)

            def spread(e):
                if e >= 2:
                    pe.wait_ge(S["weighted"], e - 1)
                for i in range(4):
                    last = nc.tensor.transpose(bank(2 + (e & 1), (1, TT), off=TT * i),
                                               v(lg, E8 * i + e, (0, C), parts=TT),
                                               cv("ident", (1, TT), parts=TT))
                last.then_inc(S["c_ready"], 1)

            def down(k, e, at):
                t = E8 * k + e
                if e == 0:
                    if at:
                        pe.wait_ge(S["y_evac"], k)
                    mm(bank(4, (1, Q)), b2s[:], v(combt, k * Q, (1, Q)),
                       start=True, stop=False, skip_group_check=True).then_inc(S["y_done"], 1)
                pe.wait_ge(S["weighted"], t + 1)
                mm(bank(4, (1, Q)), v(w2s, e * C, (1, C)), hw[e & 1], start=False, stop=(e == E8 - 1),
                   skip_group_check=True).then_inc(S["y_done"], 1)

            for e in range(E8):
                up(0, e, 0)
            pe.wait_ge(S["gelu_done"], E8)
            pe.wait_ge(S["route"], NROUTE)
            spread(0)
            spread(1)
            for t in range(NT):
                if t == 0:
                    pe.wait_ge(S["normed"], 2 * NQ)
                last = nc.tensor.transpose(bank(4 + t // 4, (1, TT), off=TT * (t % 4), parts=E8),
                                           v(lg, 8 * t, (1, 8), parts=TT),
                                           cv("ident", (1, TT), parts=TT))
                if t % 4 == 3:
                    last.then_inc(S["comb_t"], 1)
            pe.wait_ge(S["comb_copied"], NQ)
            for e in range(E8):
                if 1 <= e < E8 - 1:
                    spread(e + 1)
                if e == E8 - 2:
                    pe.wait_ge(S["normed"], 2 * NQ)
                if e >= E8 - 2:
                    up(1, e - (E8 - 2), 1)
                down(0, e, 0)

            def chunk(k, last):
                for e in range(E8):
                    if e < E8 - 2:
                        up(k, e + 2, 1)
                    elif not last:
                        up(k + 1, e - (E8 - 2), 1)
                    down(k, e, 1)

            with pe.Fori(1, NQ - 1) as k:
                chunk(k, False)
            chunk(NQ - 1, True)

        def normalise(dve, n0, k, cen, dst):
            c = slice(k * Q, (k + 1) * Q)
            dve.wait_ge(S["rstd_spread"], n0 + k + 1)
            nc.vector.tensor_tensor(dst[:, c], cen[:, c], bank(4 + k, (1, Q)), ALU.mult).then_inc(S["normed"], 1)

        def norm_vector(dve, n0, src, cen, dst, chunks):
            for k in range(NQ):
                c = slice(k * Q, (k + 1) * Q)
                dve.wait_ge(S["mean_ready"], n0 + k + 1)
                nc.vector.tensor_tensor(cen[:, c], src[:, c], bank(k, (1, Q)), ALU.subtract).then_inc(S["centred"], 1)
            dve.wait_ge(S["std_ready"], n0 // NQ + 1)
            nc.vector.reciprocal(v(stat, NT, (1, NT), parts=TT), v(stat, 0, (1, NT), parts=TT)).then_inc(S["rstd_ready"], 1)
            for k in range(chunks):
                normalise(dve, n0, k, cen, dst)

        @block.vector
        def _(dve):
            tt = nc.vector.tensor_tensor
            nc.vector.memset(mean_w[:], 1.0 / C).then_inc(S["const_set"], 1)
            nc.vector.memset(epst[:, 0:1], 1e-6).then_inc(S["const_set"], 1)
            nc.vector.memset(epst[:, 1:2], 1e-5).then_inc(S["const_set"], 1)
            nc.vector.memset(b2s[:], 0.0).then_inc(S["const_set"], 1)
            for i in range(2):
                nc.vector.memset(sc[i][:], NEG)
                nc.vector.memset(pmax[i][:], 0.0)
                nc.vector.memset(dsm[i][:], 0.0).then_inc(S["dsm_zero"], 1)
            dve.wait_ge(S["x_in"], 16 * NQ)
            norm_vector(dve, 0, xt, tok, xln, NQ)
            dve.wait_ge(S["w_q"], 64)
            nc.vector.tensor_scalar(bqr[:], bqr[:], HC ** -0.5, None, ALU.mult).then_inc(S["bq_scaled"], 1)
            dve.wait_ge(S["bq_scaled"], 1)

            def rotated_q(k):
                dve.wait_ge(S["qr_ready"], k + 1)
                nc.vector.scalar_tensor_tensor(v(qrot, k * Q, (SZ, 10), (1, SZ)), bank(4 + k, (SZ, 10), (1, SZ)), HC ** -0.5,
                                               v(bqr, 10 * k, (1, 10), (0, SZ)), ALU.mult, ALU.add
                                               ).then_inc(S["qr_copied"], 1)

            rotated_q(0)
            for cc in range(HC):
                dve.wait_ge(gk_in[cc % NG], g_loaded(cc))
                if cc >= 4 and cc % 2 == 0:
                    dve.wait_ge(S["kacc"], cc // 2 - 1)
                if cc >= 3 and cc % 2:
                    dve.wait_ge(S["kpair"], cc // 2)
                for k in range(NQ):
                    dve.wait_ge(S["pq_ready"], NQ * cc + k + 1)
                    nc.vector.scalar_tensor_tensor(v(prod[cc & 3], k * Q, (SZ, 10), (1, SZ)), bank(k, (SZ, 10), (1, SZ)),
                                                   bqs[:, cc:cc + 1], v(gk[cc % NG], cc + 10 * k * PS, (PS, 10), (1, SZ)),
                                                   ALU.add, ALU.mult).then_inc(S["kprod"], 1)
                for k in ROTATED_WITH.get(cc, ()):
                    rotated_q(k)
                if cc & 1:
                    a, b = prod[cc & 2], prod[(cc & 2) + 1]
                    dve.wait_ge(S["kprod"], NQ * (cc + 1))
                    tt(a[:], a[:], b[:], ALU.add).then_inc(S["kpair"], 1)

            def boundary_probs(j, o):
                x = px(j, o)
                dve.wait_ge(S["hot"], x + 1)
                nc.vector.tensor_reduce(v(ebd, x, (SZ, SZ)), v(hotp[o & 1], 0, (8, SZ), (1, 8)), AX, ALU.add
                                        ).then_inc(S["eb_red"], 1)

            def evacuate(j, o, at):
                x = px(j, o)
                if at is None or at >= 2:
                    dve.wait_ge(S["shifted"], x - 1)
                for b, (y0, y1, _) in enumerate(YB):
                    dve.wait_ge(S["scores_done"], 3 * x + b + 1)
                    n = y1 - y0
                    tt(v(sc[o & 1], SC * y0, (SC, n), (1, GW)), bank(b, (SW, n), (1, GW), off=SL),
                       cv("neg", (0, n), (1, GW)), ALU.add).then_inc(S["scores_evac"], 1)

            def maxima_waits(j, o):
                x = px(j, o)
                dve.wait_ge(S["scores_evac"], 3 * x + 3)
                dve.wait_ge(S["boundary_in"], x + 1)

            def maxima(j, o, at):
                x = px(j, o)
                nc.vector.copy_predicated(v(sc[o & 1], 0, (SC, SZ), (1, 8)),
                                          cv("hot", (0, SZ), (1, 8)).bitcast(I32),
                                          v(sbx[o & 1], 0, (1, SZ), (0, 8))).then_inc(S["scores_full"], 1)
                dve.wait_ge(S["scores_full"], x + 1)
                if at is None or at >= 2:
                    dve.wait_ge(S["max_t"], x - 1)
                nc.vector.tensor_reduce(v(pmax[o & 1], 0, (8, SZ), (1, 8)), v(sc[o & 1], 0, (SC, SZ), (1, 8), (8, 4)),
                                        AX, ALU.max).then_inc(S["part_max"], 1)

            def column(j, o, at, o_max):
                x = px(j, o)
                if at is None or at + 1 < SZ:
                    maxima_waits(j, o_max)
                dve.wait_ge(S["max_t"], x + 1)
                if at is None or at >= 1:
                    dve.wait_ge(S["max_bc"], x)
                nc.vector.tensor_reduce(cmax[:], bank(4, (C, 3), (1, C)), AX, ALU.max).then_inc(S["col_max"], 1)

            def shift(j, o, at):
                x = px(j, o)
                dve.wait_ge(S["max_bc"], x + 1)
                dve.wait_ge(S["scores_full"], x + 1)
                if at is None or at >= 2:
                    dve.wait_ge(S["exps"], x - 1)
                a, b = gb[o & 1], sc[o & 1]
                tt(v(a, 0, (GW, SZ), (8, 3), (1, 8)), v(b, 0, (SC, SZ), (8, 3), (1, 8)),
                   bank(5, (8, SZ), (0, 3), (1, 8)), ALU.subtract)
                tt(v(a, 24, (GW, SZ), (1, GW - 24)), v(b, 24, (SC, SZ), (1, GW - 24)),
                   bank(5, (8, SZ), (1, GW - 24)), ALU.subtract).then_inc(S["shifted"], 1)

            def weigh(j, o, at):
                x = px(j, o)
                dve.wait_ge(S["exps"], x + 1)
                dve.wait_ge(S["mask_ready"], 4 * x + 4)
                if at is None or at >= 2:
                    dve.wait_ge(S["av_done"], x - 1)
                p_, e_, m_ = pm[o & 1], ex[o & 1], mx[o & 1]
                tt(v(p_, PL, (HC * PW + 1, 2), (PW, HC), (1, GW)), v(e_, 0, (HC * GW, 2), (GW, HC), (1, GW)),
                   v(m_, 0, (HC * GW, 2), (GW, HC), (1, GW)), ALU.mult)
                tt(v(p_, PL + 2 * HC * PW + 2, (PW, 8), (1, GW)), v(e_, 2 * HC * GW, (GW, 8), (1, GW)),
                   v(m_, 2 * HC * GW, (GW, 8), (1, GW)), ALU.mult).then_inc(S["masked"], 1)

            def pick_out(j, o, at):
                x = px(j, o)
                dve.wait_ge(S["av_done"], x + 1)
                if at is None or at >= 1:
                    dve.wait_ge(S["fd_ready"], x)
                tt(osel[:], bank(7, (1, NPS * SZ)), cv("slot_o"), ALU.mult).then_inc(S["o_used"], 1)

            def pick_sum(j, o):
                x = px(j, o)
                dve.wait_ge(S["o_used"], x + 1)
                nc.vector.tensor_reduce(v(frot, x, (SZ, SZ)), v(osel, 0, (NPS, SZ), (1, NPS)), AX, ALU.add
                                        ).then_inc(S["fd_ready"], 1)

            def denominators(j, o):
                x = px(j, o)
                dve.wait_ge(S["den_done"], x + 1)
                nc.vector.tensor_reduce(v(den, 3 * x, (1, 3)), bank(6, (C, 3), (1, C)), AX, ALU.add
                                        ).then_inc(S["den_summed"], 1)

            dve.wait_ge(S["zero_buf"], 6)

            def step(j, o, at):
                if on(at, -2):
                    shift(j, o - 2, None if at is None else at - 2)
                if on(at, 0):
                    evacuate(j, o, at)
                if on(at, -5):
                    pick_out(j, o - 5, None if at is None else at - 5)
                if on(at, -4):
                    boundary_probs(j, o - 4)
                    denominators(j, o - 4)
                if on(at, -5):
                    pick_sum(j, o - 5)
                if on(at, -1):
                    column(j, o - 1, None if at is None else at - 1, o)
                elif on(at, 0):
                    maxima_waits(j, o)
                if on(at, 0):
                    maxima(j, o, at)
                if on(at, -3):
                    weigh(j, o - 3, None if at is None else at - 3)
                if at == SZ + 3:
                    dve.wait_ge(S["eb_red"], SZ)
                    dve.wait_ge(S["eb_mask"], 1)
                    for k in range(NQ):
                        c = slice(k * Q, (k + 1) * Q)
                        tt(ebd[:, c], ebd[:, c], qrot[:, c], ALU.mult).then_inc(S["eb_masked"], 1)
            nc.vector.memset(rt[:], 0.0).then_inc(S["rden"], 1)
            steps(dve, step)

            dve.wait_ge(S["den_summed"], SZ)
            dve.wait_ge(S["rden"], 1)
            nc.vector.reciprocal(v(rt, 0, (3, SZ), (1, 2)), v(den, 0, (3, SZ), (1, 2)))
            nc.vector.reciprocal(v(rt, 2, (3, SZ), parts=64), v(den, 2, (3, SZ), parts=64)).then_inc(S["rden"], 1)
            for cc in range(HC):
                dve.wait_ge(gv_in[cc % NG], g_loaded(cc))
                if cc >= 2:
                    dve.wait_ge(S["vacc"], cc - 1)
                for k in range(NQ):
                    dve.wait_ge(S["eb_perm"], k + 1)
                    tt(v(pr[cc & 1], k * Q, (SZ, 10), (1, SZ)), bank(k, (SZ, 10), (1, SZ)),
                       v(gv[cc % NG], cc + 10 * k * PS, (PS, 10), (1, SZ)), ALU.mult).then_inc(S["vprod"], 1)
                if cc == 2:
                    dve.wait_ge(S["rden"], 2)
                    for i, n in enumerate((HC, HC, 8)):
                        tt(v(rexp, i * HC * SZ, (SZ, n), (1, SZ)), v(rt, i, (0, n), (3, SZ)),
                           cv("row_of", (1, n), (0, SZ)), ALU.mult).then_inc(S["rexp_ready"], 1)
            dve.wait_ge(S["nat_in"], 16 * len(ROT))
            dve.wait_ge(S["vacc"], HC)
            for k in range(NQ):
                c = slice(k * Q, (k + 1) * Q)
                tt(sbd[:, c], sbd[:, c], bank(4 + k, (1, Q)), ALU.add).then_inc(S["zsum"], 1)
            for k in range(NQ):
                c = slice(k * Q, (k + 1) * Q)
                dve.wait_ge(S["zsum"], k + 1)
                dve.wait_ge(S["r_nat"], k + 1)
                tt(frot[:, c], sbd[:, c], bank(k, (1, Q)), ALU.mult).then_inc(S["att_nat"], 1)
            for k in range(NQ):
                c = slice(k * Q, (k + 1) * Q)
                dve.wait_ge(S["proj_done"], k + 1)
                nc.vector.scalar_tensor_tensor(xt[:, c], bank(k, (1, Q)), bp[:, 0:1], xt[:, c], ALU.add, ALU.add
                                               ).then_inc(S["resid"], 1)
            dve.wait_ge(S["resid"], NQ)
            norm_vector(dve, NQ, xt, tok, xln, 0)

            count = [0]

            def link(ins, last=False, chunk=None):
                count[0] += 1
                ins.then_inc(S["route"], 1)
                if chunk is not None:
                    normalise(dve, NQ, chunk, tok, xln)
                if not last:
                    dve.wait_ge(S["route"], count[0])

            col = lambda i, bc=False: v(lg, 11 * NT * 8 + i * NT, (1, NT), *([(0, 8)] if bc else []), parts=TT)
            iota = cv("iota", (0, NT), (1, 8), parts=TT)
            red = lambda o, i, op: nc.vector.tensor_reduce(o, i, AX, op)
            dve.wait_ge(S["logit_ready"], 1)
            dve.wait_ge(S["rstd_ready"], 2)
            link(tt(lgv(8), bank(3, (8, NT), (1, 8), parts=TT), v(stat, NT, (1, NT), (0, 8), parts=TT), ALU.mult))
            lb = lgv(8)
            link(red(col(0), lb, ALU.max))
            link(tt(lgv(1), lb, col(0, True), ALU.subtract), chunk=0)
            dve.wait_ge(S["comb_ready"], 1)
            link(red(col(1), lgv(1), ALU.add))
            link(nc.vector.reciprocal(col(2), col(1)), chunk=1)
            link(tt(lgv(2), lgv(1), col(2, True), ALU.mult), chunk=2)
            for n, (p, eq, oh, top) in enumerate(((lgv(2), lgv(3), lgv(4), 3), (lgv(5), lgv(6), lgv(7), 4))):
                link(red(col(top), p, ALU.max))
                link(tt(eq, p, col(top, True), ALU.is_equal))
                link(nc.vector.scalar_tensor_tensor(eq, eq, -8.0, iota, ALU.mult, ALU.add))
                link(red(col(5 + n), eq, ALU.min))
                link(nc.vector.tensor_scalar(col(5 + n), col(5 + n), 8.0, None, ALU.add))
                link(tt(oh, iota, col(5 + n, True), ALU.is_equal))
                if n == 0:
                    link(nc.vector.scalar_tensor_tensor(lgv(5), oh, -2.0, p, ALU.mult, ALU.add))
            link(tt(col(1), col(3), col(4), ALU.add), chunk=3)
            link(tt(lgv(4), lgv(4), col(3, True), ALU.mult))
            link(tt(lgv(7), lgv(7), col(4, True), ALU.mult))
            link(tt(lgv(4), lgv(4), lgv(7), ALU.add))
            link(nc.vector.tensor_scalar(col(1), col(1), 1e-12, None, ALU.max))
            link(nc.vector.reciprocal(col(2), col(1)))
            link(tt(lgv(0), lgv(4), col(2, True), ALU.mult), last=True)
            assert count[0] == NROUTE, count[0]

            def weighted(k, e, at, weight):
                t = E8 * k + e
                dve.wait_ge(S["gelu_done"], t + 1)
                if at == 0:
                    dve.wait_ge(S["c_ready"], t + 1)
                if e >= 2:
                    dve.wait_ge(S["y_done"], (E8 + 1) * k + e)
                elif at:
                    dve.wait_ge(S["y_done"], (E8 + 1) * k + e - 1)
                tt(hw[e & 1], hb[e], weight, ALU.mult
                   ).then_inc(S["weighted"], 1)

            def finish(k):
                dve.wait_ge(S["y_done"], (E8 + 1) * k + E8 + 1)
                tt(v(tok, k * Q, (1, Q)), v(xt, k * Q, (1, Q)), bank(4, (1, Q)), ALU.add).then_inc(S["y_evac"], 1)

            for e in range(E8):
                weighted(0, e, 0, bank(2 + (e & 1), (1, Q)))
            finish(0)
            for j in range(NQ - 2):
                dve.wait_ge(weights_in[j], 16)
                for e in range(E8):
                    weighted(j + 1, e, 1, weight_slab(j, e))
                finish(j + 1)
            dve.wait_ge(weights_in[NQ - 2], 32)
            for e in range(E8):
                weighted(NQ - 1, e, 1, weight_last(e))
            finish(NQ - 1)


def kernel(x, L0_conv_w_qkv, L0_conv_b_qkv, L0_conv_w_proj, L0_conv_b_proj,
           L0_ffn_router_w, L0_ffn_w1, L0_ffn_b1, L0_ffn_w2, L0_ffn_b2):
    import concourse.bacc as bacc
    from concourse.bass_utils import run_bass_kernel_spmd

    x, wqkv, bqkv = np.asarray(x), np.asarray(L0_conv_w_qkv), np.asarray(L0_conv_b_qkv)
    s = np.arange(C)
    co = 97 * s % C
    rot = (s[:, None] - K * np.arange(SZ)[None]) % C
    q = np.arange(C)
    grp = HC * (q % 8)[:, None] + np.arange(HC)[None]
    t = np.ascontiguousarray
    arrays = {
        "x_in": t(x.reshape(C, L)),
        "wq_t": t(wqkv[0:C].T), "wk_t": t(wqkv[C:2 * C][co].T), "wv_t": t(wqkv[2 * C:3 * C][co].T),
        "wp_t": t(np.asarray(L0_conv_w_proj).T),
        "bq_rot": t(bqkv[0:C][rot]), "bq_s": t(bqkv[0:C][grp]),
        "bkv": t(np.stack([bqkv[C:2 * C][co], bqkv[2 * C:3 * C][co]], 1)),
        "bproj": t(np.asarray(L0_conv_b_proj).reshape(C, 1)),
        "rw_t": t(np.asarray(L0_ffn_router_w).T),
        "w1": t(np.asarray(L0_ffn_w1)), "b1_t": t(np.asarray(L0_ffn_b1).T),
        "w2": t(np.asarray(L0_ffn_w2)), "b2": t(np.asarray(L0_ffn_b2)),
        "ctab": CTAB,
    }
    nc = bacc.Bacc("TRN2", target_bir_lowering=False, num_devices=1)
    args = [nc.dram_tensor(n, list(a.shape), F32, kind="ExternalInput").ap() for n, a in arrays.items()]
    out = nc.dram_tensor("out", [C, L], F32, kind="ExternalOutput").ap()
    program(nc, *args, out)
    got = run_bass_kernel_spmd(nc, [arrays], core_ids=[0]).results[0]["out"]
    return got.reshape(1, C, SZ, SZ)
```
